# Optimizing a Trainium2 kernel written in Bass

```python
import numpy as np
import jax
import jax.numpy as jnp

def _softmax(x, axis=-1):
    return jax.nn.softmax(x, axis=axis)

def _gelu(x):
    return jax.nn.gelu(x, approximate=True)

def _silu(x):
    return jax.nn.silu(x)

def _sigmoid(x):
    return jax.nn.sigmoid(x)

def _layernorm(x, axis=-1, eps=1e-05):
    m = jnp.mean(x, axis=axis, keepdims=True)
    v = jnp.var(x, axis=axis, keepdims=True)
    return (x - m) / jnp.sqrt(v + eps)

def _scatter_add(tgt, idx, src, axis=0):
    return tgt.at[idx].add(src)

def _segment_sum(src, seg, n):
    return jax.ops.segment_sum(src, seg, n)
kernel_name = 'mk_xattn_ffn_d1_seqx_r8_b472e4'

def setup_inputs(seed: int=0):
    np.random.seed(seed)
    _w = jnp.asarray

    def _rec_inputs():
        import jax
        import jax.numpy as jnp
        _rk = jax.random.key(seed)
        x = 7.22e-05 + 1 * jax.random.normal(jax.random.fold_in(_rk, 1), (16, 100, 128), jnp.float32)
        _lenS = 100 - jax.random.randint(jax.random.fold_in(_rk, 7), (16,), 0, max(1, 100 // 4) + 1, jnp.int32)
        _lenS2 = 1444 - jax.random.randint(jax.random.fold_in(_rk, 8), (16,), 0, max(1, 1444 // 4) + 1, jnp.int32)
        _ctx_1024P = jax.random.normal(jax.random.fold_in(_rk, 11), (16, 16, 128), jnp.float32)
        _ctx_1024c = jax.random.dirichlet(jax.random.fold_in(_rk, 511), 0.3 * jnp.ones((16,), jnp.float32), (16, 1444))
        _ctx_1024t = jnp.einsum('bsk,bkd->bsd', _ctx_1024c, _ctx_1024P)
        _ctx_1024t = _ctx_1024t * jax.lax.rsqrt(jnp.mean(jnp.square(_ctx_1024t)) + 1e-12) * 0.953939
        ctx_1024 = -0.000514642 + 1.00011 * (_ctx_1024t + 0.3 * jax.random.normal(jax.random.fold_in(_rk, 611), (16, 1444, 128), jnp.float32))
        return (x, ctx_1024)
    x, ctx_1024 = _rec_inputs()

    def _L0_xattn_setup():
        import jax, jax.numpy as jnp
        import numpy as np
        B, L_ENC, L_DEC, D = (16, 64, 128, 128)
        key = jax.random.key(seed)
        k1, k2, k3, k4, k5, k6 = jax.random.split(key, 6)
        encoder_hc = jax.random.normal(k1, (B, L_ENC, D), dtype=jnp.float32)
        decoder_hq = jax.random.normal(k2, (B, L_DEC, D), dtype=jnp.float32)
        w_sim = jax.random.normal(k3, (3 * D,), dtype=jnp.float32) * 0.02
        b_sim = jax.random.normal(k4, (1,), dtype=jnp.float32) * 0.02
        W_qv = jax.random.normal(k5, (4 * D, D), dtype=jnp.float32) * 0.02
        b_qv = jax.random.normal(k6, (D,), dtype=jnp.float32) * 0.02
        return {'encoder_hc': encoder_hc, 'decoder_hq': decoder_hq, 'w_sim': w_sim, 'b_sim': b_sim, 'W_qv': W_qv, 'b_qv': b_qv}
    _L0_xattn_all = _L0_xattn_setup()
    _L0_xattn_in = {k: v for k, v in _L0_xattn_all.items() if k in ('w_sim', 'b_sim', 'W_qv', 'b_qv')}
    del _L0_xattn_all

    def _L0_ffn_setup():
        import jax, jax.numpy as jnp
        import numpy as np
        D = 128
        H = 512
        E = 64
        K = 3
        B, S = (2, 256)
        C = 64
        key = jax.random.key(seed)
        ks = jax.random.split(key, 6)
        s = 0.02
        return {'x': jax.random.normal(ks[0], (B, S, D), jnp.float32), 'gate_w': jax.random.normal(ks[1], (D, E), jnp.float32) * s, 'gate_b': jnp.zeros((E,), jnp.float32), 'w1': jax.random.normal(ks[2], (E, D, H), jnp.float32) * s, 'b1': jnp.zeros((E, H), jnp.float32), 'w2': jax.random.normal(ks[3], (E, H, D), jnp.float32) * s, 'b2': jnp.zeros((E, D), jnp.float32)}
    _L0_ffn_all = _L0_ffn_setup()
    _L0_ffn_in = {k: v for k, v in _L0_ffn_all.items() if k in ('gate_w', 'gate_b', 'w1', 'b1', 'w2', 'b2')}
    del _L0_ffn_all
    return {'x': x, 'ctx_1024': ctx_1024, 'L0_xattn_w_sim': _L0_xattn_in['w_sim'], 'L0_xattn_b_sim': _L0_xattn_in['b_sim'], 'L0_xattn_W_qv': _L0_xattn_in['W_qv'], 'L0_xattn_b_qv': _L0_xattn_in['b_qv'], 'L0_ffn_gate_w': _L0_ffn_in['gate_w'], 'L0_ffn_gate_b': _L0_ffn_in['gate_b'], 'L0_ffn_w1': _L0_ffn_in['w1'], 'L0_ffn_b1': _L0_ffn_in['b1'], 'L0_ffn_w2': _L0_ffn_in['w2'], 'L0_ffn_b2': _L0_ffn_in['b2']}

def reference(x, ctx_1024, L0_xattn_w_sim, L0_xattn_b_sim, L0_xattn_W_qv, L0_xattn_b_qv, L0_ffn_gate_w, L0_ffn_gate_b, L0_ffn_w1, L0_ffn_b1, L0_ffn_w2, L0_ffn_b2):
    import jax
    import jax.numpy as jnp

    def _L0_xattn_ref(encoder_hc, decoder_hq, w_sim, b_sim, W_qv, b_qv):
        import jax, jax.numpy as jnp
        import numpy as np
        B, L_ENC, L_DEC, D = (16, 64, 128, 128)
        d = encoder_hc.shape[-1]
        w1, w2, w3 = (w_sim[:d], w_sim[d:2 * d], w_sim[2 * d:])
        Sim = (encoder_hc @ w1)[:, :, None] + (decoder_hq @ w2)[:, None, :] + jnp.einsum('bid,bjd->bij', encoder_hc * w3, decoder_hq) + b_sim[0]
        A = jax.nn.softmax(Sim, axis=2)
        hq_hat = jnp.einsum('bij,bjd->bid', A, decoder_hq)
        Batt = jax.nn.softmax(jnp.max(Sim, axis=2), axis=1)
        hc_bar = jnp.einsum('bi,bid->bd', Batt, encoder_hc)[:, None, :]
        hc_hat = jnp.broadcast_to(hc_bar, encoder_hc.shape)
        feats = jnp.concatenate([encoder_hc, hq_hat, encoder_hc * hq_hat, encoder_hc * hc_hat], axis=-1)
        hcq = feats @ W_qv + b_qv
        return hcq

    def _L0_ffn_ref(x, gate_w, gate_b, w1, b1, w2, b2):
        import jax, jax.numpy as jnp
        import numpy as np
        D = 128
        H = 512
        E = 64
        K = 3
        B, S = (2, 256)
        C = 64
        xf = x.reshape(-1, D)
        T = xf.shape[0]
        logits = xf @ gate_w + gate_b
        top_l, top_i = jax.lax.top_k(logits, K)
        gates = jax.nn.softmax(top_l, axis=-1)
        fe = top_i.reshape(-1)
        fg = gates.reshape(-1)
        tok = jnp.repeat(jnp.arange(T), K)
        oh = jax.nn.one_hot(fe, E, dtype=jnp.int32)
        pos = (jnp.cumsum(oh, axis=0) * oh).sum(-1) - 1
        valid = pos < C
        buf = jnp.zeros((E, C, D), x.dtype).at[fe, pos].set(xf[tok], mode='drop')
        h = jax.nn.gelu(jnp.einsum('ecd,edh->ech', buf, w1) + b1[:, None, :], approximate=False)
        y = jnp.einsum('ech,ehd->ecd', h, w2) + b2[:, None, :]
        rows = y[fe, jnp.minimum(pos, C - 1)] * (fg * valid.astype(x.dtype))[:, None]
        out = jnp.zeros_like(xf).at[tok].add(rows)
        return out.reshape(x.shape)
    x = x + _L0_xattn_ref(_layernorm(x, axis=-1), ctx_1024, L0_xattn_w_sim, L0_xattn_b_sim, L0_xattn_W_qv, L0_xattn_b_qv)
    x = x + _L0_ffn_ref(_layernorm(x, axis=-1), L0_ffn_gate_w, L0_ffn_gate_b, L0_ffn_w1, L0_ffn_b1, L0_ffn_w2, L0_ffn_b2)
    return x

_drawn_inputs = setup_inputs


def setup_inputs(seed=0):
    import zlib

    import numpy as np

    out = dict(_drawn_inputs(seed))
    spreads = {'L0_ffn_gate_b': (0.0, 0.1), 'L0_ffn_b1': (0.0, 0.758), 'L0_ffn_b2': (0.0, 0.1)}
    factors = {}
    for name, (base, spread) in spreads.items():
        noise = np.random.default_rng([zlib.crc32(name.encode()), seed]).standard_normal(out[name].shape)
        drawn = base * np.exp(spread * noise) if base else spread * noise
        out[name] = jnp.asarray(drawn.astype(out[name].dtype))
    for name, factor in factors.items():
        out[name] = (out[name] * factor).astype(out[name].dtype)
    return out
```

```python
from contextlib import ExitStack

import concourse.bass as bass
from concourse import mybir

ALU = mybir.AluOpType
ACT = mybir.ActivationFunctionType
AX = mybir.AxisListType
F32 = mybir.dt.float32
BF16 = mybir.dt.bfloat16
I32 = mybir.dt.int32
U32 = mybir.dt.uint32

P = 128
TOPK = 3
CAP = 64
EPS = 1e-5
BANK = 512
STEP_RING = 3
W_RING = 16
G_RING = 8
Y_RING = 4
FFN_UNROLL = 4


def build_xattn_moe(nc, x, ctx, w_sim, b_sim, w_qv, b_qv, gate_w, gate_b, w1, b1, w2, b2, out):
    B, L, D = x.shape
    S = ctx.shape[1]
    E, _, H = w1.shape
    T = B * L
    MAIN = S // P
    REM = S - MAIN * P
    TILES = MAIN + 1
    GROUPS = 3
    PER = TILES // GROUPS
    NP = E // 2
    HC = H // P
    TRASH = (E - 1) * CAP + T
    SPARE = T * TOPK
    assert D == P and TILES == GROUPS * PER and NP == 2 * W_RING and 2 * CAP == P

    xln_d = nc.dram_tensor("xln_scratch", (T, D), F32)
    table_d = nc.dram_tensor("table_scratch", (TRASH + T * TOPK, 4), F32)
    y_d = nc.dram_tensor("y_scratch", (SPARE + E * CAP, D), F32)

    with ExitStack() as stack:
        def sb(name, shape, dt=F32):
            return stack.enter_context(nc.sbuf_tensor(name, shape, dt))

        def sem(name):
            return stack.enter_context(nc.semaphore(name))

        def sems(name, n):
            return [sem(f"{name}{i}") for i in range(n)]

        ident = sb("ident", [P, P])
        ones = sb("ones", [P, P])
        earlier = sb("earlier", [L, L], BF16)
        ones_h = sb("ones_h", [L, L], BF16)
        expert_no = sb("expert_no", [L, E])
        expert_i = sb("expert_i", [L, E], I32)
        trash_row = sb("trash_row", [L, B * TOPK])
        trash_i = sb("trash_i", [L, B * TOPK], I32)
        neg_half = sb("neg_half", [L, B])
        wsim = sb("wsim", [P, 3])
        neg_w1 = sb("neg_w1", [P, P])
        neg_b = sb("neg_b", [P, 1])
        bsim = sb("bsim", [P, 1])
        wqv = sb("wqv", [P, 4, D])
        bqv = sb("bqv", [L, D])
        gatew = sb("gatew", [P, E])
        gateb = sb("gateb", [L, E])
        b1_rows = sb("b1_rows", [E, H])
        b1T = sb("b1T", [P, E * HC])
        b2_rows = sb("b2_rows", [E, D])
        b2T = sb("b2T", [P, E])
        xs = sb("xs", [L, B, D])
        x2 = sb("x2", [L, B, D])
        stats = sb("stats", [L, B, 6])
        moments = sb("moments", [L, B, 2])
        var_eps = sb("var_eps", [L, B])
        rstd = sb("rstd", [L, B])
        rec = sb("rec", [L, B * TOPK, 4])
        rec_now = sb("rec_now", [L, STEP_RING, TOPK, 4])
        rec_i = sb("rec_i", [L, B * TOPK, 2], I32)
        cx = sb("cx", [P, STEP_RING, TILES, D + 1])
        cxT = sb("cxT", [P, S])
        enc = sb("enc", [L, D])
        encT = sb("encT", [P, STEP_RING, L])
        query = sb("query", [P, L])
        maxes = sb("maxes", [P, L])
        row_max = sb("row_max", [L, 1])
        neg_diag = sb("neg_diag", [L, L])
        shift = sb("shift", [P, 2 * L])
        shifted = sb("shifted", [P, TILES * L])
        probs = sb("probs", [P, TILES * L])
        inv_sum = sb("inv_sum", [L, 1])
        hq = sb("hq", [L, D])
        hqT = sb("hqT", [P, L])
        enc_hq = sb("enc_hq", [P, L])
        neg_r = sb("neg_r", [P, L])
        neg_rmax = sb("neg_rmax", [P, 1])
        batt = sb("batt", [P, L])
        batt_sum = sb("batt_sum", [P, 1])
        hc_junk = sb("hc_junk", [P, L])
        hc_raw = sb("hc_raw", [P, 1])
        hc_bar = sb("hc_bar", [P, 1])
        batt_inv = sb("batt_inv", [P, 1])
        enc_hc = sb("enc_hc", [P, L])
        st2 = sb("st2", [L, 6])
        mv2 = sb("mv2", [L, 2])
        var_eps2 = sb("var_eps2", [L, 1])
        rstd2 = sb("rstd2", [L, 1])
        xln = sb("xln", [L, STEP_RING, D])
        xlnT = sb("xlnT", [P, L])
        logits = sb("logits", [L, E])
        top = sb("top", [L, 8])
        top_ix = sb("top_ix", [L, 8], U32)
        top_no = sb("top_no", [L, TOPK])
        pick0 = sb("pick0", [L, E])
        pick01 = sb("pick01", [L, E])
        mask = sb("mask", [L, E], BF16)
        seen = sb("seen", [L, STEP_RING, E], BF16)
        pos_junk = sb("pos_junk", [L, TOPK, E])
        pos = sb("pos", [L, TOPK])
        top_d = sb("top_d", [L, TOPK])
        gate_e = sb("gate_e", [L, TOPK])
        gate_sum = sb("gate_sum", [L, 1])
        gate_inv = sb("gate_inv", [L, 1])
        slot_b = sb("slot_b", [L, TOPK])
        over = sb("over", [L, TOPK])
        slot = sb("slot", [L, STEP_RING, TOPK], I32)
        tab0 = sb("tab0", [NP, P, 4])
        tab0_i = sb("tab0_i", [NP, P], I32)
        token_ix = sb("token_ix", [P, NP], I32)
        y_row = sb("y_row", [P, NP], I32)
        gates = sb("gates", [P, NP])
        gather_ix = sb("gather_ix", [P, G_RING], I32)
        scatter_ix = sb("scatter_ix", [P, Y_RING], I32)
        wring = sb("wring", [P, W_RING, 2, 2, HC * D])
        spent = cx[:, :, :, :].rearrange("p k t d -> p (k t d)")

        def reuse(first, count, width):
            return spent[:, first:first + count * width].rearrange("p (n w) -> p n w", n=count)

        xg = reuse(0, G_RING, D)
        xgT = reuse(G_RING * D, 2, P)
        hidden = reuse(G_RING * D + 2 * P, 2, BANK)
        yT = reuse(G_RING * D + 2 * P + 2 * BANK, 2, P)
        yg = reuse(G_RING * D + 4 * P + 2 * BANK, Y_RING, D)
        zeros = sb("zeros", [P, 400])
        yk = wring[0:L, 0:3].rearrange("p s a e n -> p (s a e n)").rearrange("p (b n) -> p b n", b=B)

        bank = [stack.enter_context(nc.psum_tensor(f"bank{i}", [P, BANK], F32)) for i in range(3, 8)]
        sim = stack.enter_context(nc.psum_tensor("sim", [P, GROUPS, BANK], F32))
        turnA, turnB, attn_bank, max_bank, misc = bank

        const_in = sem("const_in")
        x_in = sem("x_in")
        x2_in = sem("x2_in")
        bias_in = sem("bias_in")
        ctx_in = sems("ctx_in", STEP_RING)
        w_first = sem("w_first")
        w_next = sems("w_next", W_RING)
        filled = sem("filled")
        zeroed = sem("zeroed")
        table_init = sem("table_init")
        y_init = sem("y_init")
        consts = sem("consts")
        halves = sem("halves")
        built = sem("built")
        neg_w1_ok = sem("neg_w1_ok")
        x_bias = sem("x_bias")
        b_turned = sem("b_turned")
        b_kept = sem("b_kept")
        stats_ok = sem("stats_ok")
        moments_ok = sem("moments_ok")
        rstd_ok = sem("rstd_ok")
        normed = sem("normed")
        enc_ok = sem("enc_ok")
        enc_turned = sem("enc_turned")
        encT_ok = sem("encT_ok")
        query_ok = sem("query_ok")
        ctx_turned = sems("ctx_turned", GROUPS)
        cxT_ok = sems("cxT_ok", GROUPS)
        sim_ok = sem("sim_ok")
        maxes_ok = sem("maxes_ok")
        max_turned = sem("max_turned")
        row_max_ok = sem("row_max_ok")
        diag_ok = sem("diag_ok")
        spread = sem("spread")
        shift_ok = sem("shift_ok")
        shifted_ok = sems("shifted_ok", GROUPS)
        probs_ok = sem("probs_ok")
        attn_ok = sem("attn_ok")
        inv_ok = sem("inv_ok")
        hq_ok = sem("hq_ok")
        hq_turned = sem("hq_turned")
        hqT_ok = sem("hqT_ok")
        enc_hq_ok = sem("enc_hq_ok")
        neg_r_ok = sem("neg_r_ok")
        neg_rmax_ok = sem("neg_rmax_ok")
        batt_ok = sem("batt_ok")
        hc_raw_ok = sem("hc_raw_ok")
        hc_ok = sem("hc_ok")
        batt_inv_ok = sem("batt_inv_ok")
        enc_hc_ok = sem("enc_hc_ok")
        qv_ok = sem("qv_ok")
        x2_ok = sem("x2_ok")
        st2_ok = sem("st2_ok")
        mv2_ok = sem("mv2_ok")
        var_eps_ok = sem("var_eps_ok")
        var_eps2_ok = sem("var_eps2_ok")
        rstd2_ok = sem("rstd2_ok")
        xln_ok = sem("xln_ok")
        xln_out = sems("xln_out", STEP_RING)
        xln_turned = sem("xln_turned")
        xlnT_ok = sem("xlnT_ok")
        logits_raw = sem("logits_raw")
        logits_ok = sem("logits_ok")
        top_ok = sem("top_ok")
        top_ix_ok = sem("top_ix_ok")
        top_no_ok = sem("top_no_ok")
        pick0_ok = sem("pick0_ok")
        pick01_ok = sem("pick01_ok")
        mask_ok = sem("mask_ok")
        seen_ok = sem("seen_ok")
        counted = sem("counted")
        pos_ok = sem("pos_ok")
        top_d_ok = sem("top_d_ok")
        gate_e_ok = sem("gate_e_ok")
        gate_inv_ok = sem("gate_inv_ok")
        gate_ok = sem("gate_ok")
        slot_b_ok = sem("slot_b_ok")
        over_ok = sem("over_ok")
        slot_ok = sem("slot_ok")
        rec_now_ok = sem("rec_now_ok")
        rec_out = sems("rec_out", STEP_RING)
        table_in = sem("table_in")
        table_turned = sem("table_turned")
        table_ok = sem("table_ok")
        first_ix_ok = sem("first_ix_ok")
        gather_ix_ok = sem("gather_ix_ok")
        scatter_ix_ok = sem("scatter_ix_ok")
        gathered = sems("gathered", G_RING)
        xg_turned = sem("xg_turned")
        xgT_ok = sem("xgT_ok")
        up_ok = sem("up_ok")
        biased = sem("biased")
        hidden_ok = sem("hidden_ok")
        down_ok = sem("down_ok")
        yT_ok = sem("yT_ok")
        y_turned = sem("y_turned")
        yg_ok = sem("yg_ok")
        y_out = sems("y_out", Y_RING)
        y_in = sems("y_in", 4)
        sum_part = sem("sum_part")
        sum_ok = sem("sum_ok")
        out_sem = sem("out_sem")

        LAST_STEP = B + 1
        PEEL = 2 + STEP_RING
        LOOPS = (B - 2 - PEEL) // STEP_RING
        TAIL = range(PEEL + LOOPS * STEP_RING, LAST_STEP + 1)

        def there(b):
            return not isinstance(b, int) or 0 <= b < B

        def past(s, n):
            return not isinstance(s, int) or s >= n

        def in_loop(s):
            return not isinstance(s, int)

        def steps(eng, step):
            for r in range(-1, PEEL):
                step(0, r)
            with eng.Fori(1, 1 + LOOPS) as turn:
                for r in range(PEEL - STEP_RING, PEEL):
                    step(turn, r)
            for s in TAIL:
                step(0, s)

        def there_pair(j):
            return not isinstance(j, int) or 0 <= j < NP

        def ffn_steps(eng, step):
            for u in range(-3, FFN_UNROLL):
                step(0, u)
            with eng.Fori(1, NP // FFN_UNROLL - 1) as turn:
                for u in range(FFN_UNROLL):
                    step(turn, u)
            for j in range(NP - FFN_UNROLL, NP):
                step(0, j)

        up_bank = [sim[:, 0], sim[:, 1]]
        down_bank = [sim[:, 2], turnA]
        xg_bank = [turnB, attn_bank]
        y_bank = [max_bank, misc]

        def tile_cols(slot_no):
            start = 0 if slot_no == 0 else REM + (slot_no - 1) * P
            return slice(start, start + P)

        def rows_of(slot_no):
            return REM if slot_no == 0 else P

        block = stack.enter_context(nc.Block())

        @block.sync
        def _(sp):
            def load_ctx(turn, r):
                k = r % STEP_RING
                b = STEP_RING * turn + r
                sp.dma_start(cx[:, k, 1:TILES, 0:D],
                             ctx[bass.ds(b, 1), 0:MAIN * P, :].rearrange("o (p t) d -> p (o t) d", t=MAIN)
                             ).then_inc(ctx_in[k], 16)
                sp.dma_start(cx[0:REM, k, 0, 0:D],
                             ctx[bass.ds(b, 1), MAIN * P:S, :].rearrange("o p d -> p (o d)")
                             ).then_inc(ctx_in[k], 16)

            def load_weights(pair, k, done):
                sp.dma_start(wring[:, bass.ds(k, 1), 0].rearrange("p o e n -> p (o e) n"),
                             w1[bass.ds(2 * pair, 2)].rearrange("e d h -> d e h")).then_inc(done, 16)
                sp.dma_start(wring[:, bass.ds(k, 1), 1].rearrange("p o e n -> p (o e) n"),
                             w2[bass.ds(2 * pair, 2)].rearrange("e (p c) n -> p e (c n)", c=HC)
                             ).then_inc(done, 16)

            sp.dma_start(xs[:, :, :], x.rearrange("b l d -> l b d")).then_inc(x_in, 16)
            sp.dma_start(x2[:, :, :], x.rearrange("b l d -> l b d")).then_inc(x2_in, 16)
            load_ctx(0, 0)
            sp.dma_start(wsim[:, :], w_sim.rearrange("(c d) -> d c", d=D), allow_slow_non_contiguous=True).then_inc(const_in, 16)
            sp.dma_start(bsim[:, :], b_sim.partition_broadcast(P)).then_inc(const_in, 16)
            sp.dma_start(wqv[:, :, :], w_qv.rearrange("(c d) n -> d c n", d=D)).then_inc(const_in, 16)
            sp.dma_start(bqv[:, :], b_qv.partition_broadcast(L)).then_inc(const_in, 16)
            sp.dma_start(gatew[:, :], gate_w).then_inc(const_in, 16)
            sp.dma_start(gateb[:, :], gate_b.partition_broadcast(L)).then_inc(const_in, 16)
            sp.dma_start(b1_rows[:, :], b1).then_inc(bias_in, 16)
            sp.dma_start(b2_rows[:, :], b2).then_inc(bias_in, 16)
            load_ctx(0, 1)
            sp.wait_ge(filled, 1)
            sp.dma_start(table_d[0:E * CAP, :].rearrange("(j s) f -> j s f", s=P), tab0[:, :, :]
                         ).then_inc(table_init, 16)
            load_weights(0, 0, w_first)
            sp.wait_ge(zeroed, 1)
            sp.dma_start(y_d[0:SPARE, :].rearrange("r d -> (r d)").rearrange("(p n w) -> p n w", p=P, w=400),
                         zeros[:, :].unsqueeze(1).to_broadcast([P, SPARE * D // P // 400, 400])
                         ).then_inc(y_init, 16)

            def step(turn, r):
                s = STEP_RING * turn + r
                if there(s - 2):
                    sp.wait_ge(xln_ok, s - 1)
                    sp.dma_start(xln_d[bass.ds((s - 2) * L, L), :], xln[:, (r - 2) % STEP_RING, :]
                                 ).then_inc(xln_out[(r - 2) % STEP_RING], 16)
                if there(s + 2):
                    if past(s, 1):
                        sp.wait_ge(attn_ok, s)
                    if past(s, 0):
                        load_ctx(turn, r + 2)
                    load_weights(s + 2, s + 2, w_first)

            steps(sp, step)

            for k in range(W_RING):
                sp.wait_ge(down_ok, k + 1)
                load_weights(W_RING + k, k, w_next[k])

            for k in range(Y_RING):
                sp.wait_ge(y_out[k], 16 * (NP // Y_RING))
            for c in range(4):
                rows = y_d[c * 4 * L * TOPK:(c + 1) * 4 * L * TOPK, :].rearrange(
                    "(b l k) d -> l b (k d)", b=4, l=L)
                sp.dma_start(yk[0:96, 4 * c:4 * c + 4, :], rows[0:96]).then_inc(y_in[c], 16)
                sp.dma_start(yk[96:L, 4 * c:4 * c + 4, :], rows[96:L]).then_inc(y_in[c], 16)
            for c in range(4):
                sp.wait_ge(sum_ok, c + 1)
                sp.dma_start(out[4 * c:4 * c + 4].rearrange("b l d -> l b d"), x2[:, 4 * c:4 * c + 4, :]
                             ).then_inc(out_sem, 16)
            sp.wait_ge(out_sem, 4 * 16)

        @block.gpsimd
        def _(pool):
            pool.memset(neg_half[:, :], -0.5).then_inc(halves, 1)
            pool.memset(ident[:, :], 0.0).then_inc(consts, 1)
            pool.memset(ones[:, :], 1.0).then_inc(consts, 1)
            pool.memset(earlier[:, :], 1.0).then_inc(consts, 1)
            pool.memset(ones_h[:, :], 1.0).then_inc(consts, 1)
            pool.memset(tab0[:, :, :], 0.0).then_inc(consts, 1)
            pool.memset(rec[:, :, :], 0.0).then_inc(consts, 1)
            pool.memset(seen[:, 0, :], 0.0).then_inc(consts, 1)
            pool.iota(tab0_i[:, :], pattern=[[1, P]], base=SPARE, channel_multiplier=P).then_inc(consts, 1)
            pool.iota(trash_i[:, :], pattern=[[L, B * TOPK]], base=TRASH, channel_multiplier=1).then_inc(consts, 1)
            pool.iota(expert_i[:, :], pattern=[[1, E]], base=0, channel_multiplier=0).then_inc(consts, 1)
            pool.iota(rec_i[:, :, 0].rearrange("p (b k) -> p b k", k=TOPK), pattern=[[L, B], [0, TOPK]],
                      base=0, channel_multiplier=1).then_inc(consts, 1)
            pool.iota(rec_i[:, :, 1].rearrange("p (b k) -> p b k", k=TOPK), pattern=[[L * TOPK, B], [1, TOPK]],
                      base=0, channel_multiplier=TOPK).then_inc(consts, 1)
            pool.wait_ge(consts, 12)
            pool.tensor_copy(tab0[:, :, 1], tab0_i[:, :]).then_inc(filled, 1)
            pool.affine_select(out=ident[:, :], in_=ident[:, :], compare_op=ALU.not_equal, fill=1.0,
                               base=0, pattern=[[-1, P]], channel_multiplier=1).then_inc(built, 1)
            pool.memset(cx[:, :, :, D:D + 1], 1.0).then_inc(built, 1)
            pool.affine_select(out=earlier[:, :], in_=earlier[:, :], compare_op=ALU.is_gt, fill=0.0,
                               base=0, pattern=[[1, L]], channel_multiplier=-1).then_inc(built, 1)
            pool.tensor_copy(trash_row[:, :], trash_i[:, :]).then_inc(built, 1)
            pool.tensor_copy(expert_no[:, :], expert_i[:, :]).then_inc(built, 1)
            pool.tensor_copy(rec[:, :, 0:2], rec_i[:, :, :]).then_inc(built, 1)
            pool.memset(zeros[:, :], 0.0).then_inc(zeroed, 1)
            pool.wait_ge(const_in, 6 * 16)
            pool.tensor_scalar(neg_w1[:, :], ones[:, :], wsim[:, 0:1], -1.0, ALU.mult, ALU.mult
                               ).then_inc(neg_w1_ok, 1)
            pool.tensor_scalar(neg_b[:, :], bsim[:, :], -1.0, None, ALU.mult).then_inc(neg_w1_ok, 1)

            pool.wait_ge(halves, 1)
            pool.wait_ge(var_eps_ok, 1)
            pool.tensor_tensor(rstd[:, :], var_eps[:, :], neg_half[:, :], ALU.pow).then_inc(rstd_ok, 1)
            pool.wait_ge(x2_in, 16)
            pool.tensor_tensor(x2[:, :, :], x2[:, :, :],
                               bqv[:, :].unsqueeze(1).to_broadcast([L, B, D]), ALU.add).then_inc(x_bias, 1)
            pool.wait_ge(built, 6)

            def step(turn, r):
                s = STEP_RING * turn + r
                old = (r - 2) % STEP_RING
                if there(s - 2):
                    pool.wait_ge(var_eps2_ok, s - 1)
                    pool.tensor_tensor(rstd2[:, :], var_eps2[:, :], neg_half[:, 0:1], ALU.pow).then_inc(rstd2_ok, 1)
                    pool.wait_ge(rec_out[old], 16 * TOPK * (turn + (r - 2) // STEP_RING))
                    pool.tensor_copy(rec_now[:, old], rec[:, bass.ds(TOPK * (s - 2), TOPK), :]
                                     ).then_inc(rec_now_ok, 1)
                if there(s + 1):
                    if past(s, 0):
                        pool.wait_ge(enc_turned, s + 1)
                    pool.wait_ge(normed, s + 2)
                    pool.tensor_copy(enc[:, :], xs[:, bass.ds(s + 1, 1), :].rearrange("p o d -> p (o d)")
                                     ).then_inc(enc_ok, 1)
                if there(s - 1):
                    pool.wait_ge(hc_ok, s)
                    if past(s, 2):
                        pool.wait_ge(qv_ok, s - 1)
                    pool.tensor_tensor(enc_hc[:, :], encT[:, (r - 1) % STEP_RING, :],
                                       hc_bar[:, :].to_broadcast([P, L]), ALU.mult).then_inc(enc_hc_ok, 1)
                if there(s - 2):
                    if in_loop(s):
                        pool.wait_ge(built, 6)
                    pool.wait_ge(top_ok, s - 1)
                    pool.tensor_scalar(top_d[:, :], top[:, 0:TOPK], top[:, 0:1], None, ALU.subtract
                                       ).then_inc(top_d_ok, 1)
                    pool.wait_ge(mask_ok, s - 1)
                    pool.wait_ge(seen_ok, s - 2)
                    pool.tensor_tensor(seen[:, (r - 1) % STEP_RING, :], seen[:, old, :], mask[:, :], ALU.add
                                       ).then_inc(seen_ok, 1)
                if there(s + 1):
                    if in_loop(s):
                        pool.wait_ge(built, 6)
                    pool.wait_ge(encT_ok, s + 2)
                    if past(s, 0):
                        pool.wait_ge(sim_ok, s + 1)
                    pool.tensor_scalar(query[:, :], encT[:, (r + 1) % STEP_RING, :], wsim[:, 2:3], wsim[:, 1:2],
                                       ALU.mult, ALU.add).then_inc(query_ok, 1)
                if there(s - 1):
                    pool.wait_ge(hqT_ok, s)
                    pool.tensor_tensor(enc_hq[:, :], encT[:, (r - 1) % STEP_RING, :], hqT[:, :], ALU.mult
                                       ).then_inc(enc_hq_ok, 1)
                if there(s - 2):
                    b = s - 2
                    pool.wait_ge(table_init, 16)
                    pool.wait_ge(slot_ok, b + 1)
                    pool.wait_ge(gate_ok, b + 1)
                    for k in range(TOPK):
                        pool.indirect_dma_start(
                            out=table_d[:, :], out_offset=bass.IndirectOffsetOnAxis(ap=slot[:, old, k:k + 1], axis=0),
                            in_=rec_now[:, old, k, :], in_offset=None
                        ).then_inc(rec_out[old], 16)

            steps(pool, step)

            for k in range(STEP_RING):
                pool.wait_ge(rec_out[k], 16 * TOPK * len(range(k, B, STEP_RING)))
            pool.dma_start(tab0[:, :, :], table_d[0:E * CAP, :].rearrange("(j s) f -> j s f", s=P)
                           ).then_inc(table_in, 16)
            for k in range(STEP_RING):
                pool.wait_ge(xln_out[k], 16 * len(range(k, B, STEP_RING)))
            pool.wait_ge(table_ok, 3)
            pool.wait_ge(y_init, 16)

            def gather(j, u, copied, count):
                k = u % G_RING
                pool.tensor_copy(gather_ix[:, k:k + 1], token_ix[:, bass.ds(j, 1)]).then_inc(copied, 1)
                if in_loop(j):
                    pool.wait_ge(built, 6)
                pool.wait_ge(copied, count)
                pool.indirect_dma_start(
                    out=xg[:, k, :], out_offset=None, in_=xln_d[:, :],
                    in_offset=bass.IndirectOffsetOnAxis(ap=gather_ix[:, k:k + 1], axis=0)
                ).then_inc(gathered[k], 16)

            def scatter(j, u):
                k = u % Y_RING
                pool.wait_ge(yg_ok, j + 1)
                pool.tensor_copy(scatter_ix[:, k:k + 1], y_row[:, bass.ds(j, 1)]).then_inc(scatter_ix_ok, 1)
                if in_loop(j):
                    pool.wait_ge(built, 6)
                pool.wait_ge(scatter_ix_ok, j + 1)
                pool.indirect_dma_start(
                    out=y_d[:, :], out_offset=bass.IndirectOffsetOnAxis(ap=scatter_ix[:, k:k + 1], axis=0),
                    in_=yg[:, k, :], in_offset=None).then_inc(y_out[k], 16)

            for j in range(G_RING):
                gather(j, j, first_ix_ok, j + 1)
            with pool.Fori(0, NP // G_RING - 1) as turn:
                for u in range(G_RING):
                    j = G_RING * turn + u
                    scatter(j, u)
                    pool.wait_ge(xg_turned, j + 1)
                    gather(j + G_RING, u, gather_ix_ok, j + 1)
            with pool.Fori(NP // Y_RING - G_RING // Y_RING, NP // Y_RING) as turn:
                for u in range(Y_RING):
                    scatter(Y_RING * turn + u, u)

        @block.scalar
        def _(act):
            def step(turn, r):
                s = STEP_RING * turn + r
                if there(s - 1):
                    act.wait_ge(neg_rmax_ok, s)
                    if past(s, 2):
                        act.wait_ge(enc_hc_ok, s - 1)
                    act.activation(batt[:, :], neg_r[:, :], ACT.Exp, bias=neg_rmax[:, :], scale=-1.0,
                                   accum_out=batt_sum[:, :]).then_inc(batt_ok, 1)
                    act.wait_ge(shifted_ok[GROUPS - 1], s)
                    if past(s, 2):
                        act.wait_ge(attn_ok, s - 1)
                    act.activation(probs[:, :], shifted[:, :], ACT.Exp).then_inc(probs_ok, 1)
                if there(s - 2):
                    act.wait_ge(xln_turned, s - 1)
                    act.copy(xlnT[:, :], misc[:, 0:L]).then_inc(xlnT_ok, 1)
                if there(s - 1):
                    act.wait_ge(inv_ok, s)
                    act.activation(hq[:, :], attn_bank[0:L, 0:D], ACT.Copy, scale=inv_sum[:, :]
                                   ).then_inc(hq_ok, 1)
                if there(s + 1):
                    act.wait_ge(ctx_turned[0], s + 2)
                    act.copy(cxT[:, 0:REM + 3 * P], turnA[:, 0:REM + 3 * P]).then_inc(cxT_ok[0], 1)
                if there(s):
                    act.wait_ge(spread, s + 1)
                    if past(s, 1):
                        act.wait_ge(neg_r_ok, s)
                    act.copy(shift[:, :], max_bank[:, 0:2 * L]).then_inc(shift_ok, 1)
                if there(s + 1):
                    act.wait_ge(ctx_turned[1], s + 2)
                    act.copy(cxT[:, REM + 3 * P:REM + 7 * P], turnB[:, :]).then_inc(cxT_ok[1], 1)
                    act.wait_ge(enc_turned, s + 2)
                    if past(s, 2):
                        act.wait_ge(qv_ok, s - 1)
                    act.copy(encT[:, (r + 1) % STEP_RING, :], misc[:, 0:L]).then_inc(encT_ok, 1)
                if there(s - 1):
                    act.wait_ge(hq_turned, s)
                    act.copy(hqT[:, :], attn_bank[:, 0:L]).then_inc(hqT_ok, 1)
                if there(s + 1):
                    act.wait_ge(ctx_turned[2], s + 2)
                    act.copy(cxT[:, REM + 7 * P:S], turnA[:, :]).then_inc(cxT_ok[2], 1)
                if there(s - 2):
                    act.wait_ge(top_d_ok, s - 1)
                    if past(s, 3):
                        act.wait_ge(gate_ok, s - 2)
                    act.activation(gate_e[:, :], top_d[:, :], ACT.Exp, accum_out=gate_sum[:, :]
                                   ).then_inc(gate_e_ok, 1)

            steps(act, step)

            def ffn_step(turn, u):
                j = FFN_UNROLL * turn + u
                if there_pair(j):
                    act.wait_ge(y_turned, j + 1)
                    act.wait_ge(y_out[u % Y_RING], 16 * (turn + u // Y_RING))
                    act.activation(yg[:, u % Y_RING, :], y_bank[u % 2][:, 0:D], ACT.Copy,
                                   scale=gates[:, bass.ds(j, 1)]).then_inc(yg_ok, 1)
                if there_pair(j + 2):
                    act.wait_ge(biased, j + 3)
                    act.activation(hidden[:, u % 2, :], hidden[:, u % 2, :], ACT.Gelu).then_inc(hidden_ok, 1)

            ffn_steps(act, ffn_step)

        @block.vector
        def _(dve):
            dve.wait_ge(x_in, 16)
            for b in range(B):
                dve.bn_stats(stats[:, b, :], xs[:, b, :]).then_inc(stats_ok, 1)
            for b in range(B):
                dve.wait_ge(stats_ok, b + 1)
                dve.bn_aggr(moments[:, b, :], stats[:, b, :]).then_inc(moments_ok, 1)
            dve.wait_ge(moments_ok, B)
            dve.tensor_scalar(var_eps[:, :], moments[:, :, 1], EPS, None, ALU.add).then_inc(var_eps_ok, 1)
            dve.wait_ge(rstd_ok, 1)
            for b in range(B):
                dve.tensor_scalar(xs[:, b, :], xs[:, b, :], moments[:, b, 0:1], rstd[:, b:b + 1],
                                  ALU.subtract, ALU.mult).then_inc(normed, 1)
            dve.wait_ge(built, 6)
            dve.wait_ge(neg_w1_ok, 2)

            def step(turn, r):
                s = STEP_RING * turn + r
                if there(s - 2):
                    k = (r - 2) % STEP_RING
                    dve.wait_ge(rstd2_ok, s - 1)
                    dve.wait_ge(xln_out[k], 16 * (turn + (r - 2) // STEP_RING))
                    dve.tensor_scalar(xln[:, k, :], x2[:, bass.ds(s - 2, 1), :].rearrange("p o d -> p (o d)"),
                                      mv2[:, 0:1], rstd2[:, :], ALU.subtract, ALU.mult).then_inc(xln_ok, 1)
                if there(s):
                    dve.wait_ge(sim_ok, s + 1)
                    if past(s, 1):
                        dve.wait_ge(max_turned, s)
                    dve.tensor_reduce(maxes[:, :],
                                      sim[:, :, 0:PER * L].rearrange("p g (t i) -> p i g t", t=PER),
                                      AX.XY, ALU.max).then_inc(maxes_ok, 1)
                if there(s - 1):
                    dve.wait_ge(attn_ok, s)
                    if past(s, 2):
                        dve.wait_ge(hq_ok, s - 1)
                    dve.reciprocal(inv_sum[:, :], attn_bank[0:L, D:D + 1]).then_inc(inv_ok, 1)
                if there(s - 2):
                    b = s - 2
                    dve.wait_ge(logits_raw, b + 1)
                    dve.tensor_tensor(logits[:, :], misc[0:L, 0:E], gateb[:, :], ALU.add).then_inc(logits_ok, 1)
                    if in_loop(s):
                        dve.wait_ge(built, 6)
                    dve.wait_ge(logits_ok, b + 1)
                    dve.wait_ge(top_d_ok, b)
                    dve.max(top[:, :], logits[:, :]).then_inc(top_ok, 1)
                    if in_loop(s):
                        dve.wait_ge(built, 6)
                    dve.wait_ge(top_ok, b + 1)
                    dve.max_index(top_ix[:, :], top[:, :], logits[:, :]).then_inc(top_ix_ok, 1)
                    dve.wait_ge(top_ix_ok, b + 1)
                    dve.tensor_copy(top_no[:, :], top_ix[:, 0:TOPK]).then_inc(top_no_ok, 1)
                    dve.wait_ge(top_no_ok, b + 1)
                    dve.tensor_scalar(pick0[:, :], expert_no[:, :], top_no[:, 0:1], None, ALU.is_equal
                                      ).then_inc(pick0_ok, 1)
                    dve.wait_ge(pick0_ok, b + 1)
                    dve.scalar_tensor_tensor(pick01[:, :], expert_no[:, :], top_no[:, 1:2], pick0[:, :],
                                             ALU.is_equal, ALU.add).then_inc(pick01_ok, 1)
                    dve.wait_ge(pick01_ok, b + 1)
                    dve.wait_ge(seen_ok, b)
                    dve.scalar_tensor_tensor(mask[:, :], expert_no[:, :], top_no[:, 2:3], pick01[:, :],
                                             ALU.is_equal, ALU.add).then_inc(mask_ok, 1)
                if there(s - 1):
                    dve.wait_ge(batt_ok, s)
                    if past(s, 2):
                        dve.wait_ge(enc_hc_ok, s - 1)
                    dve.tensor_tensor_reduce(hc_junk[:, :], batt[:, :], encT[:, (r - 1) % STEP_RING, :], 1.0, 0.0,
                                             ALU.mult, ALU.add, hc_raw[:, :]).then_inc(hc_raw_ok, 1)
                    dve.reciprocal(batt_inv[:, :], batt_sum[:, :]).then_inc(batt_inv_ok, 1)
                    dve.wait_ge(hc_raw_ok, s)
                    dve.wait_ge(batt_inv_ok, s)
                    dve.tensor_tensor(hc_bar[:, :], hc_raw[:, :], batt_inv[:, :], ALU.mult).then_inc(hc_ok, 1)
                if there(s):
                    dve.wait_ge(max_turned, s + 1)
                    dve.tensor_reduce(row_max[:, :], max_bank[0:L, 0:P], AX.X, ALU.max).then_inc(row_max_ok, 1)
                    dve.wait_ge(row_max_ok, s + 1)
                    dve.tensor_scalar(neg_diag[:, :], ident[0:L, 0:L], row_max[:, :], -1.0, ALU.mult, ALU.mult
                                      ).then_inc(diag_ok, 1)
                    dve.wait_ge(shift_ok, s + 1)
                    if past(s, 1):
                        dve.wait_ge(probs_ok, s)
                    for g in range(GROUPS):
                        w = PER * L
                        dve.tensor_tensor(shifted[:, g * w:(g + 1) * w].rearrange("p (t i) -> p t i", t=PER),
                                          sim[:, g, 0:w].rearrange("p (t i) -> p t i", t=PER),
                                          shift[:, 0:L].unsqueeze(1).to_broadcast([P, PER, L]),
                                          ALU.add).then_inc(shifted_ok[g], 1)
                    if past(s, 1):
                        dve.wait_ge(batt_ok, s)
                    dve.scalar_tensor_tensor(neg_r[:, :], shift[:, 0:L], neg_b[:, :], shift[:, L:2 * L],
                                             ALU.add, ALU.add).then_inc(neg_r_ok, 1)
                    dve.wait_ge(neg_r_ok, s + 1)
                    dve.tensor_reduce(neg_rmax[:, :], neg_r[:, :], AX.X, ALU.min).then_inc(neg_rmax_ok, 1)
                if there(s - 2):
                    b = s - 2
                    dve.wait_ge(counted, b + 1)
                    for k in range(TOPK):
                        dve.scalar_tensor_tensor(pos_junk[:, k, :], expert_no[:, :], top_no[:, k:k + 1],
                                                 attn_bank[0:L, 0:E], ALU.is_equal, ALU.mult,
                                                 accum_out=pos[:, k:k + 1]).then_inc(pos_ok, 1)
                    dve.wait_ge(pos_ok, TOPK * (b + 1))
                    dve.scalar_tensor_tensor(slot_b[:, :], top_no[:, :], float(CAP), pos[:, :],
                                             ALU.mult, ALU.add).then_inc(slot_b_ok, 1)
                    dve.scalar_tensor_tensor(over[:, :], pos[:, :], float(CAP),
                                             trash_row[:, bass.ds(TOPK * b, TOPK)],
                                             ALU.is_ge, ALU.mult).then_inc(over_ok, 1)
                    dve.wait_ge(slot_b_ok, b + 1)
                    dve.wait_ge(over_ok, b + 1)
                    dve.wait_ge(rec_out[(r - 2) % STEP_RING], 16 * TOPK * (turn + (r - 2) // STEP_RING))
                    dve.tensor_tensor(slot[:, (r - 2) % STEP_RING, :], slot_b[:, :], over[:, :], ALU.max
                                      ).then_inc(slot_ok, 1)
                    dve.wait_ge(gate_e_ok, b + 1)
                    dve.reciprocal(gate_inv[:, :], gate_sum[:, :]).then_inc(gate_inv_ok, 1)
                    dve.wait_ge(gate_inv_ok, b + 1)
                    dve.wait_ge(rec_now_ok, b + 1)
                    dve.tensor_scalar(rec_now[:, (r - 2) % STEP_RING, :, 2], gate_e[:, :], gate_inv[:, :], None,
                                      ALU.mult).then_inc(gate_ok, 1)
                if there(s - 1):
                    b = s - 1
                    if not past(s, 2):
                        dve.wait_ge(x_bias, 1)
                    row = x2[:, bass.ds(b, 1), :].rearrange("p o d -> p (o d)")
                    dve.wait_ge(qv_ok, b + 1)
                    dve.tensor_tensor(row, misc[0:L, 0:D], row, ALU.add).then_inc(x2_ok, 1)
                    if in_loop(s):
                        dve.wait_ge(built, 6)
                    dve.wait_ge(x2_ok, b + 1)
                    dve.bn_stats(st2[:, :], row).then_inc(st2_ok, 1)
                    if in_loop(s):
                        dve.wait_ge(built, 6)
                    dve.wait_ge(st2_ok, b + 1)
                    dve.bn_aggr(mv2[:, :], st2[:, :]).then_inc(mv2_ok, 1)
                    dve.wait_ge(mv2_ok, b + 1)
                    dve.tensor_scalar(var_eps2[:, :], mv2[:, 1:2], EPS, None, ALU.add).then_inc(var_eps2_ok, 1)


            steps(dve, step)

            dve.wait_ge(b_turned, 1)
            dve.tensor_copy(b1T[:, :].rearrange("p (e c) -> p c e", c=HC),
                            sim[:, 0, 0:HC * E].rearrange("p (c e) -> p c e", c=HC)).then_inc(b_kept, 1)
            dve.tensor_copy(b2T[:, :], sim[:, 0, HC * E:HC * E + E]).then_inc(b_kept, 1)
            dve.wait_ge(table_turned, 1)
            dve.tensor_copy(token_ix[:, :], sim[:, 1, 0:NP]).then_inc(table_ok, 1)
            dve.tensor_copy(y_row[:, :], sim[:, 1, NP:2 * NP]).then_inc(table_ok, 1)
            dve.tensor_copy(gates[:, :], sim[:, 1, 2 * NP:3 * NP]).then_inc(table_ok, 1)
            dve.wait_ge(b_kept, 2)

            def ffn_step(turn, u):
                j = FFN_UNROLL * turn + u
                if there_pair(j):
                    dve.wait_ge(down_ok, j + 1)
                    if not isinstance(j, int) or j >= 2:
                        dve.wait_ge(y_turned, j - 1)
                    dve.tensor_tensor(yT[:, u % 2, :].rearrange("p (e s) -> p e s", e=2),
                                      down_bank[u % 2][:, 0:P].rearrange("p (e s) -> p e s", e=2),
                                      b2T[:, bass.ds(2 * j, 2)].unsqueeze(2).to_broadcast([P, 2, CAP]),
                                      ALU.add).then_inc(yT_ok, 1)
                if there_pair(j + 3):
                    dve.wait_ge(xg_turned, j + 4)
                    if not isinstance(j, int) or j >= -1:
                        dve.wait_ge(up_ok, j + 2)
                    dve.tensor_copy(xgT[:, (u + 3) % 2, :], xg_bank[(u + 3) % 2][:, 0:P]).then_inc(xgT_ok, 1)
                if there_pair(j + 2):
                    dve.wait_ge(up_ok, j + 3)
                    dve.tensor_tensor(hidden[:, u % 2, :].rearrange("p (e s) -> p e s", s=CAP),
                                      up_bank[u % 2].rearrange("p (e s) -> p e s", s=CAP),
                                      b1T[:, bass.ds(2 * HC * (j + 2), 2 * HC)].unsqueeze(2)
                                      .to_broadcast([P, 2 * HC, CAP]), ALU.add).then_inc(biased, 1)

            ffn_steps(dve, ffn_step)

            for c in range(4):
                dve.wait_ge(y_in[c], 32)
                mine = x2[:, 4 * c:4 * c + 4, :]
                for k in range(TOPK):
                    if k:
                        dve.wait_ge(sum_part, 2 * c + k)
                    dve.tensor_tensor(mine, mine, yk[:, 4 * c:4 * c + 4, k * D:(k + 1) * D], ALU.add
                                      ).then_inc(sum_part if k < TOPK - 1 else sum_ok, 1)

        @block.tensor
        def _(pe):
            def turn_tiles(target, first, slots, k):
                for i in slots:
                    n = rows_of(i)
                    at = tile_cols(i).start - first
                    last = pe.transpose(target[:, at:at + n], cx[0:n, k, i, 0:D], ident[0:n, 0:n])
                return last

            def step(turn, r):
                s = STEP_RING * turn + r
                old, now, new = (r - 1) % STEP_RING, r % STEP_RING, (r + 1) % STEP_RING
                if there(s):
                    pe.wait_ge(query_ok, s + 1)
                    for g in range(GROUPS):
                        pe.wait_ge(cxT_ok[g], s + 1)
                        if past(s, 1):
                            pe.wait_ge(shifted_ok[g], s)
                        for t in range(PER):
                            last = pe.matmul(sim[:, g, t * L:(t + 1) * L], cxT[:, tile_cols(g * PER + t)],
                                             query[:, :], start=True, stop=True)
                    last.then_inc(sim_ok, 1)
                if there(s - 2):
                    pe.wait_ge(xln_ok, s - 1)
                    pe.transpose(misc[:, 0:L], xln[:, (r - 2) % STEP_RING, :], ident[0:L, 0:L]
                                 ).then_inc(xln_turned, 1)
                if there(s - 1):
                    pe.wait_ge(probs_ok, s)
                    if past(s, 3):
                        pe.wait_ge(pos_ok, TOPK * (s - 2))
                    for i in range(TILES):
                        n = rows_of(i)
                        last = pe.matmul(attn_bank[0:L, 0:D + 1], probs[0:n, i * L:(i + 1) * L],
                                         cx[0:n, old, i, :], start=(i == 0), stop=(i == TILES - 1))
                    last.then_inc(attn_ok, 1)
                if there(s - 2):
                    pe.wait_ge(xlnT_ok, s - 1)
                    pe.matmul(misc[0:L, 0:E], xlnT[:, :], gatew[:, :], start=True, stop=True
                              ).then_inc(logits_raw, 1)
                if there(s):
                    pe.wait_ge(maxes_ok, s + 1)
                    if past(s, 1):
                        pe.wait_ge(shift_ok, s)
                    pe.transpose(max_bank[0:L, 0:P], maxes[:, :], ident[:, :]).then_inc(max_turned, 1)
                if there(s + 1):
                    pe.wait_ge(ctx_in[new], 32 * (turn + (r + 1) // STEP_RING + 1))
                    if past(s, 0):
                        pe.wait_ge(cxT_ok[2], s + 1)
                    turn_tiles(turnA, 0, (1, 2, 3, 0), new).then_inc(ctx_turned[0], 1)
                    if past(s, 0):
                        pe.wait_ge(cxT_ok[1], s + 1)
                    turn_tiles(turnB, REM + 3 * P, range(PER, 2 * PER), new).then_inc(ctx_turned[1], 1)
                if there(s):
                    pe.wait_ge(diag_ok, s + 1)
                    pe.matmul(max_bank[:, 0:L], ones[0:L, :], neg_diag[:, :], start=True, stop=True)
                    pe.matmul(max_bank[:, L:2 * L], neg_w1[:, :], encT[:, now, :], start=True, stop=True
                              ).then_inc(spread, 1)
                if there(s + 1):
                    pe.wait_ge(enc_ok, s + 2)
                    if there(s - 2):
                        pe.wait_ge(logits_ok, s - 1)
                    pe.transpose(misc[:, 0:L], enc[:, :], ident[0:L, 0:L]).then_inc(enc_turned, 1)
                if there(s - 1):
                    pe.wait_ge(hq_ok, s)
                    pe.transpose(attn_bank[:, 0:L], hq[:, :], ident[0:L, 0:L]).then_inc(hq_turned, 1)
                if there(s + 1):
                    pe.wait_ge(cxT_ok[0], s + 2)
                    turn_tiles(turnA, REM + 7 * P, range(2 * PER, TILES), new).then_inc(ctx_turned[2], 1)
                if there(s - 2):
                    pe.wait_ge(mask_ok, s - 1)
                    if past(s, 3):
                        pe.wait_ge(seen_ok, s - 2)
                    if there(s - 1):
                        pe.wait_ge(hqT_ok, s)
                    pe.matmul(attn_bank[0:L, 0:E], earlier[:, :], mask[:, :], start=True, stop=False)
                    pe.matmul(attn_bank[0:L, 0:E], ones_h[:, :], seen[:, (r - 2) % STEP_RING, :],
                              start=False, stop=True).then_inc(counted, 1)
                if there(s - 1):
                    if there(s + 1):
                        pe.wait_ge(encT_ok, s + 2)
                    pe.matmul(misc[0:L, 0:D], encT[:, old, :], wqv[:, 0, :], start=True, stop=False)
                    pe.wait_ge(hqT_ok, s)
                    pe.matmul(misc[0:L, 0:D], hqT[:, :], wqv[:, 1, :], start=False, stop=False)
                    pe.wait_ge(enc_hc_ok, s)
                    pe.matmul(misc[0:L, 0:D], enc_hc[:, :], wqv[:, 3, :], start=False, stop=False)
                    pe.wait_ge(enc_hq_ok, s)
                    pe.matmul(misc[0:L, 0:D], enc_hq[:, :], wqv[:, 2, :], start=False, stop=True
                              ).then_inc(qv_ok, 1)

            pe.wait_ge(built, 6)
            pe.wait_ge(neg_w1_ok, 2)
            steps(pe, step)

            pe.wait_ge(bias_in, 32)
            for c in range(HC):
                pe.transpose(sim[:, 0, c * E:(c + 1) * E],
                             b1_rows[:, :].rearrange("e (p c) -> e c p", c=HC)[:, c, :], ident[0:E, 0:E])
            pe.transpose(sim[:, 0, HC * E:HC * E + E], b2_rows[:, :], ident[0:E, 0:E]).then_inc(b_turned, 1)
            pe.wait_ge(table_in, 16)
            for f in range(3):
                last = pe.transpose(sim[:, 1, f * NP:(f + 1) * NP], tab0[:, :, f], ident[0:NP, 0:NP])
            last.then_inc(table_turned, 1)
            pe.wait_ge(b_kept, 2)
            pe.wait_ge(table_ok, 3)

            def turn_tokens(turn, u):
                j = W_RING * turn + u
                pe.wait_ge(gathered[u % G_RING], 16 * (W_RING // G_RING * turn + u // G_RING + 1))
                if not isinstance(j, int) or j >= 2:
                    pe.wait_ge(xgT_ok, j - 1)
                pe.transpose(xg_bank[u % 2][:, 0:P], xg[:, u % G_RING, :], ident[:, :]).then_inc(xg_turned, 1)

            def up(turn, u):
                j = W_RING * turn + u
                k = u % W_RING
                pe.wait_ge(w_next[k], 32 * (turn + u // W_RING))
                pe.wait_ge(xgT_ok, j + 1)
                if not isinstance(j, int) or j >= 2:
                    pe.wait_ge(biased, j - 1)
                for e in range(2):
                    w = wring[:, k, 0, e].rearrange("p (m c) -> p c m", c=HC)
                    for c in range(HC):
                        at = (e * HC + c) * CAP
                        last = pe.matmul(up_bank[u % 2][:, at:at + CAP], w[:, c, :],
                                         xgT[:, u % 2, e * CAP:(e + 1) * CAP], start=True, stop=True)
                last.then_inc(up_ok, 1)

            def down(turn, u):
                j = W_RING * turn + u
                k = u % W_RING
                pe.wait_ge(hidden_ok, j + 1)
                if not isinstance(j, int) or j >= 2:
                    pe.wait_ge(yT_ok, j - 1)
                for e in range(2):
                    for c in range(HC):
                        at = (e * HC + c) * CAP
                        last = pe.matmul(down_bank[u % 2][:, e * CAP:(e + 1) * CAP],
                                         wring[:, k, 1, e, c * D:(c + 1) * D],
                                         hidden[:, u % 2, at:at + CAP], start=(c == 0), stop=(c == HC - 1))
                last.then_inc(down_ok, 1)

            def turn_y(turn, u):
                j = W_RING * turn + u
                pe.wait_ge(yT_ok, j + 1)
                if not isinstance(j, int) or j >= 2:
                    pe.wait_ge(yg_ok, j - 1)
                pe.transpose(y_bank[u % 2][:, 0:D], yT[:, u % 2, :], ident[:, :]).then_inc(y_turned, 1)

            pe.wait_ge(w_first, 32 * W_RING)
            turn_tokens(0, 0)
            turn_tokens(0, 1)
            up(0, 0)
            turn_tokens(0, 2)
            up(0, 1)

            def ffn_step(turn, u, more):
                down(turn, u)
                if more > 2:
                    turn_tokens(turn, u + 3)
                if more > 1:
                    up(turn, u + 2)
                turn_y(turn, u)

            for turn in range(NP // W_RING):
                for u in range(W_RING):
                    ffn_step(turn, u, NP - 1 - (W_RING * turn + u))


_INS = ['x', 'ctx_1024', 'L0_xattn_w_sim', 'L0_xattn_b_sim', 'L0_xattn_W_qv', 'L0_xattn_b_qv', 'L0_ffn_gate_w',
        'L0_ffn_gate_b', 'L0_ffn_w1', 'L0_ffn_b1', 'L0_ffn_w2', 'L0_ffn_b2']


def kernel(**inputs):
    import numpy as np
    import concourse.bacc as bacc
    from concourse.bass_utils import run_bass_kernel_spmd

    nc = bacc.Bacc("TRN2", target_bir_lowering=False, num_devices=1)
    arrays, args = {}, []
    for name in _INS:
        a = np.ascontiguousarray(inputs[name])
        arrays[f"in_{name}"] = a
        args.append(nc.dram_tensor(f"in_{name}", a.shape, mybir.dt.from_np(a.dtype), kind="ExternalInput").ap())
    shape = inputs['x'].shape
    args.append(nc.dram_tensor("out_0", shape, F32, kind="ExternalOutput").ap())
    build_xattn_moe(nc, *args)
    result = run_bass_kernel_spmd(nc, [arrays], core_ids=[0])
    return result.results[0]["out_0"]
```

```python
from contextlib import ExitStack

import concourse.bass as bass
from concourse import mybir

ALU = mybir.AluOpType
ACT = mybir.ActivationFunctionType
AX = mybir.AxisListType
F32 = mybir.dt.float32
BF16 = mybir.dt.bfloat16
I32 = mybir.dt.int32
U32 = mybir.dt.uint32

P = 128
TOPK = 3
CAP = 64
EPS = 1e-5
BANK = 512
STEP_RING = 3
W_RING = 16
G_RING = 8
Y_RING = 4
FFN_UNROLL = 4


def build_xattn_moe(nc, x, ctx, w_sim, b_sim, w_qv, b_qv, gate_w, gate_b, w1, b1, w2, b2, out):
    B, L, D = x.shape
    S = ctx.shape[1]
    E, _, H = w1.shape
    T = B * L
    MAIN = S // P
    REM = S - MAIN * P
    TILES = MAIN + 1
    GROUPS = 3
    PER = TILES // GROUPS
    NP = E // 2
    HC = H // P
    TRASH = (E - 1) * CAP + T
    SPARE = T * TOPK
    assert D == P and TILES == GROUPS * PER and NP == 2 * W_RING and 2 * CAP == P

    xln_d = nc.dram_tensor("xln_scratch", (T, D), F32)
    table_d = nc.dram_tensor("table_scratch", (TRASH + T * TOPK, 4), F32)
    y_d = nc.dram_tensor("y_scratch", (SPARE + E * CAP, D), F32)

    with ExitStack() as stack:
        def sb(name, shape, dt=F32):
            return stack.enter_context(nc.sbuf_tensor(name, shape, dt))

        def sem(name):
            return stack.enter_context(nc.semaphore(name))

        def sems(name, n):
            return [sem(f"{name}{i}") for i in range(n)]

        ident = sb("ident", [P, P])
        ones = sb("ones", [P, P])
        earlier = sb("earlier", [L, L], BF16)
        ones_h = sb("ones_h", [L, L], BF16)
        expert_no = sb("expert_no", [L, E])
        expert_i = sb("expert_i", [L, E], I32)
        trash_row = sb("trash_row", [L, B * TOPK])
        trash_i = sb("trash_i", [L, B * TOPK], I32)
        neg_half = sb("neg_half", [L, B])
        wsim = sb("wsim", [P, 3])
        neg_w1 = sb("neg_w1", [P, P])
        neg_b = sb("neg_b", [P, 1])
        bsim = sb("bsim", [P, 1])
        wqv = sb("wqv", [P, 4, D])
        bqv = sb("bqv", [L, D])
        gatew = sb("gatew", [P, E])
        gateb = sb("gateb", [L, E])
        b1_rows = sb("b1_rows", [E, H])
        b1T = sb("b1T", [P, E * HC])
        b2_rows = sb("b2_rows", [P, D])
        xs = sb("xs", [L, B, D])
        x2 = sb("x2", [L, B, D])
        stats = sb("stats", [L, B, 6])
        moments = sb("moments", [L, B, 2])
        var_eps = sb("var_eps", [L, B])
        rstd = sb("rstd", [L, B])
        rec = sb("rec", [L, B * TOPK, 4])
        rec_now = sb("rec_now", [L, STEP_RING, TOPK, 4])
        rec_i = sb("rec_i", [L, B * TOPK, 2], I32)
        cx = sb("cx", [P, STEP_RING, TILES, D + 1])
        cxT = sb("cxT", [P, S])
        enc = sb("enc", [L, D])
        encT = sb("encT", [P, STEP_RING, L])
        query = sb("query", [P, L])
        maxes = sb("maxes", [P, L])
        row_max = sb("row_max", [L, 1])
        neg_diag = sb("neg_diag", [L, L])
        shift = sb("shift", [P, 2 * L])
        shifted = sb("shifted", [P, TILES * L])
        probs = sb("probs", [P, TILES * L])
        inv_sum = sb("inv_sum", [L, 1])
        hq = sb("hq", [L, D])
        hqT = sb("hqT", [P, L])
        enc_hq = sb("enc_hq", [P, L])
        neg_r = sb("neg_r", [P, L])
        neg_rmax = sb("neg_rmax", [P, 1])
        batt = sb("batt", [P, L])
        batt_sum = sb("batt_sum", [P, 1])
        hc_junk = sb("hc_junk", [P, L])
        hc_raw = sb("hc_raw", [P, 1])
        batt_inv = sb("batt_inv", [P, 1])
        enc_hc = sb("enc_hc", [P, L])
        st2 = sb("st2", [L, 6])
        mv2 = sb("mv2", [L, 2])
        var_eps2 = sb("var_eps2", [L, 1])
        rstd2 = sb("rstd2", [L, 1])
        xln = sb("xln", [L, STEP_RING, D])
        xlnT = sb("xlnT", [P, L])
        logits = sb("logits", [L, E])
        top = sb("top", [L, 8])
        top_ix = sb("top_ix", [L, 8], U32)
        top_no = sb("top_no", [L, TOPK])
        pick0 = sb("pick0", [L, E])
        pick01 = sb("pick01", [L, E])
        mask = sb("mask", [L, E], BF16)
        seen = sb("seen", [L, STEP_RING, E], BF16)
        pos_junk = sb("pos_junk", [L, TOPK, E])
        pos = sb("pos", [L, TOPK])
        top_d = sb("top_d", [L, TOPK])
        gate_e = sb("gate_e", [L, TOPK])
        gate_sum = sb("gate_sum", [L, 1])
        gate_inv = sb("gate_inv", [L, 1])
        slot_b = sb("slot_b", [L, TOPK])
        over = sb("over", [L, TOPK])
        slot = sb("slot", [L, STEP_RING, TOPK], I32)
        tab0 = sb("tab0", [NP, P, 4])
        tab0_i = sb("tab0_i", [NP, P], I32)
        token_ix = sb("token_ix", [P, NP], I32)
        y_row = sb("y_row", [P, NP], I32)
        gates = sb("gates", [P, NP])
        wring = sb("wring", [P, W_RING, 2, 2, HC * D])
        spent = cx[:, :, :, :].rearrange("p k t d -> p (k t d)")

        def reuse(first, count, width):
            return spent[:, first:first + count * width].rearrange("p (n w) -> p n w", n=count)

        xg = reuse(0, G_RING, D)
        xgT = reuse(G_RING * D, 2, P)
        hidden = reuse(G_RING * D + 2 * P, 2, BANK)
        yg = reuse(G_RING * D + 2 * P + 2 * BANK, Y_RING, D)
        zeros = sb("zeros", [P, 400])
        yk = wring[0:L, 0:3].rearrange("p s a e n -> p (s a e n)").rearrange("p (b n) -> p b n", b=B)

        bank = [stack.enter_context(nc.psum_tensor(f"bank{i}", [P, BANK], F32)) for i in range(3, 8)]
        sim = stack.enter_context(nc.psum_tensor("sim", [P, GROUPS, BANK], F32))
        turnA, turnB, attn_bank, max_bank, misc = bank

        const_in = sem("const_in")
        wsim_in = sem("wsim_in")
        x0_in = sem("x0_in")
        x_in = sem("x_in")
        ident_ok = sem("ident_ok")
        cleared = sem("cleared")
        x2_in = sem("x2_in")
        bias_in = sem("bias_in")
        ctx_in = sems("ctx_in", STEP_RING)
        w_first = sem("w_first")
        w_next = sems("w_next", W_RING)
        filled = sem("filled")
        zeroed = sem("zeroed")
        table_init = sem("table_init")
        y_init = sem("y_init")
        consts = sem("consts")
        halves = sem("halves")
        built = sem("built")
        neg_w1_ok = sem("neg_w1_ok")
        x_bias = sem("x_bias")
        b_turned = sem("b_turned")
        b_kept = sem("b_kept")
        b2_padded = sem("b2_padded")
        stats_ok = sem("stats_ok")
        moments_ok = sem("moments_ok")
        rstd_ok = sem("rstd_ok")
        enc_ok = sem("enc_ok")
        enc_turned = sem("enc_turned")
        encT_ok = sem("encT_ok")
        query_ok = sem("query_ok")
        ctx_turned = sems("ctx_turned", GROUPS)
        cxT_ok = sems("cxT_ok", GROUPS)
        sim_ok = sem("sim_ok")
        maxes_ok = sem("maxes_ok")
        max_turned = sem("max_turned")
        row_max_ok = sem("row_max_ok")
        diag_ok = sem("diag_ok")
        spread = sem("spread")
        shift_ok = sem("shift_ok")
        shifted_ok = sems("shifted_ok", GROUPS)
        probs_ok = sem("probs_ok")
        attn_ok = sem("attn_ok")
        inv_ok = sem("inv_ok")
        hq_ok = sem("hq_ok")
        hq_turned = sem("hq_turned")
        hqT_ok = sem("hqT_ok")
        enc_hq_ok = sem("enc_hq_ok")
        neg_r_ok = sem("neg_r_ok")
        neg_rmax_ok = sem("neg_rmax_ok")
        batt_ok = sem("batt_ok")
        hc_raw_ok = sem("hc_raw_ok")
        batt_inv_ok = sem("batt_inv_ok")
        enc_hc_ok = sem("enc_hc_ok")
        qv_ok = sem("qv_ok")
        x2_ok = sem("x2_ok")
        st2_ok = sem("st2_ok")
        mv2_ok = sem("mv2_ok")
        var_eps_ok = sem("var_eps_ok")
        var_eps2_ok = sem("var_eps2_ok")
        rstd2_ok = sem("rstd2_ok")
        xln_ok = sem("xln_ok")
        xln_out = sems("xln_out", STEP_RING)
        xln_turned = sem("xln_turned")
        xlnT_ok = sem("xlnT_ok")
        logits_raw = sem("logits_raw")
        logits_ok = sem("logits_ok")
        top_ok = sem("top_ok")
        top_ix_ok = sem("top_ix_ok")
        top_no_ok = sem("top_no_ok")
        pick0_ok = sem("pick0_ok")
        pick01_ok = sem("pick01_ok")
        mask_ok = sem("mask_ok")
        seen_ok = sem("seen_ok")
        counted = sem("counted")
        pos_ok = sem("pos_ok")
        top_d_ok = sem("top_d_ok")
        gate_e_ok = sem("gate_e_ok")
        gate_inv_ok = sem("gate_inv_ok")
        gate_ok = sem("gate_ok")
        slot_b_ok = sem("slot_b_ok")
        over_ok = sem("over_ok")
        slot_ok = sem("slot_ok")
        rec_now_ok = sem("rec_now_ok")
        rec_out = sems("rec_out", STEP_RING)
        table_in = sem("table_in")
        table_turned = sem("table_turned")
        table_ok = sem("table_ok")
        gathered = sems("gathered", G_RING)
        xg_turned = sem("xg_turned")
        xgT_ok = sem("xgT_ok")
        up_ok = sem("up_ok")
        biased = sem("biased")
        hidden_ok = sem("hidden_ok")
        down_ok = sem("down_ok")
        yg_ok = sem("yg_ok")
        y_out = sems("y_out", Y_RING)
        y_in = sems("y_in", 4)
        sum_part = sem("sum_part")
        sum_ok = sem("sum_ok")
        out_sem = sem("out_sem")

        LAST_STEP = B + 2
        PEEL = 3 + STEP_RING
        LOOPS = (B - 2 - PEEL) // STEP_RING
        TAIL = range(PEEL + LOOPS * STEP_RING, LAST_STEP + 1)

        def there(b):
            return not isinstance(b, int) or 0 <= b < B

        def past(s, n):
            return not isinstance(s, int) or s >= n

        def in_loop(s):
            return not isinstance(s, int)

        def steps(eng, step):
            for r in range(-1, PEEL):
                step(0, r)
            with eng.Fori(1, 1 + LOOPS) as turn:
                for r in range(PEEL - STEP_RING, PEEL):
                    step(turn, r)
            for s in TAIL:
                step(0, s)

        def there_pair(j):
            return not isinstance(j, int) or 0 <= j < NP

        def ffn_steps(eng, step):
            for u in range(-3, FFN_UNROLL):
                step(0, u)
            with eng.Fori(1, NP // FFN_UNROLL - 1) as turn:
                for u in range(FFN_UNROLL):
                    step(turn, u)
            for j in range(NP - FFN_UNROLL, NP):
                step(0, j)

        up_bank = [[sim[:, 0], sim[:, 1]], [sim[:, 2], turnA[:, :]]]
        down_bank = [turnB, attn_bank]
        xg_bank = [max_bank, misc]

        def tile_cols(slot_no):
            start = 0 if slot_no == 0 else REM + (slot_no - 1) * P
            return slice(start, start + P)

        def rows_of(slot_no):
            return REM if slot_no == 0 else P

        block = stack.enter_context(nc.Block())

        @block.sync
        def _(sp):
            def load_ctx(turn, r):
                k = r % STEP_RING
                b = STEP_RING * turn + r
                sp.dma_start(cx[:, k, 1:TILES, 0:D],
                             ctx[bass.ds(b, 1), 0:MAIN * P, :].rearrange("o (p t) d -> p (o t) d", t=MAIN)
                             ).then_inc(ctx_in[k], 16)
                sp.dma_start(cx[0:REM, k, 0, 0:D],
                             ctx[bass.ds(b, 1), MAIN * P:S, :].rearrange("o p d -> p (o d)")
                             ).then_inc(ctx_in[k], 16)

            def load_weights(pair, k, done):
                sp.dma_start(wring[:, bass.ds(k, 1), 0].rearrange("p o e n -> p (o e) n"),
                             w1[bass.ds(2 * pair, 2)].rearrange("e d h -> d e h")).then_inc(done, 16)
                sp.dma_start(wring[:, bass.ds(k, 1), 1].rearrange("p o e n -> p (o e) n"),
                             w2[bass.ds(2 * pair, 2)].rearrange("e (p c) n -> p e (c n)", c=HC)
                             ).then_inc(done, 16)

            sp.dma_start(xs[:, 0, :], x[0]).then_inc(x0_in, 16)
            load_ctx(0, 0)
            sp.dma_start(wsim[:, :], w_sim.rearrange("(c d) -> d c", d=D), allow_slow_non_contiguous=True
                         ).then_inc(wsim_in, 16)
            sp.dma_start(bsim[:, :], b_sim.partition_broadcast(P)).then_inc(wsim_in, 16)
            sp.dma_start(xs[:, 1:B, :], x[1:B].rearrange("b l d -> l b d")).then_inc(x_in, 16)
            load_ctx(0, 1)
            sp.dma_start(bqv[:, :], b_qv.partition_broadcast(L)).then_inc(const_in, 16)
            sp.dma_start(x2[:, :, :], x.rearrange("b l d -> l b d")).then_inc(x2_in, 16)
            sp.dma_start(wqv[:, :, :], w_qv.rearrange("(c d) n -> d c n", d=D)).then_inc(const_in, 16)
            sp.dma_start(gatew[:, :], gate_w).then_inc(const_in, 16)
            sp.dma_start(gateb[:, :], gate_b.partition_broadcast(L)).then_inc(const_in, 16)
            sp.dma_start(b1_rows[:, :], b1).then_inc(bias_in, 16)
            sp.dma_start(b2_rows[0:E, :], b2).then_inc(bias_in, 16)
            sp.wait_ge(filled, 1)
            sp.dma_start(table_d[0:E * CAP, :].rearrange("(j s) f -> j s f", s=P), tab0[:, :, :]
                         ).then_inc(table_init, 16)
            load_weights(0, 0, w_first)
            sp.wait_ge(zeroed, 1)
            sp.dma_start(y_d[0:SPARE, :].rearrange("r d -> (r d)").rearrange("(p n w) -> p n w", p=P, w=400),
                         zeros[:, :].unsqueeze(1).to_broadcast([P, SPARE * D // P // 400, 400])
                         ).then_inc(y_init, 16)

            def step(turn, r):
                s = STEP_RING * turn + r
                if there(s - 2):
                    sp.wait_ge(xln_ok, s - 1)
                    sp.dma_start(xln_d[bass.ds((s - 2) * L, L), :], xln[:, (r - 2) % STEP_RING, :]
                                 ).then_inc(xln_out[(r - 2) % STEP_RING], 16)
                if there(s + 2):
                    if past(s, 1):
                        sp.wait_ge(attn_ok, s)
                    if past(s, 0):
                        load_ctx(turn, r + 2)
                    load_weights(s + 2, s + 2, w_first)

            steps(sp, step)

            for k in range(W_RING):
                sp.wait_ge(down_ok, k + 1)
                load_weights(W_RING + k, k, w_next[k])

            for k in range(Y_RING):
                sp.wait_ge(y_out[k], 16 * (NP // Y_RING))
            for c in range(4):
                rows = y_d[c * 4 * L * TOPK:(c + 1) * 4 * L * TOPK, :].rearrange(
                    "(b l k) d -> l b (k d)", b=4, l=L)
                sp.dma_start(yk[0:96, 4 * c:4 * c + 4, :], rows[0:96]).then_inc(y_in[c], 16)
                sp.dma_start(yk[96:L, 4 * c:4 * c + 4, :], rows[96:L]).then_inc(y_in[c], 16)
            for c in range(4):
                sp.wait_ge(sum_ok, c + 1)
                sp.dma_start(out[4 * c:4 * c + 4].rearrange("b l d -> l b d"), x2[:, 4 * c:4 * c + 4, :]
                             ).then_inc(out_sem, 16)
            sp.wait_ge(out_sem, 4 * 16)

        @block.gpsimd
        def _(pool):
            pool.memset(ident[:, :], 0.0).then_inc(cleared, 1)
            pool.memset(neg_half[:, :], -0.5).then_inc(halves, 1)
            pool.wait_ge(cleared, 1)
            pool.affine_select(out=ident[:, :], in_=ident[:, :], compare_op=ALU.not_equal, fill=1.0,
                               base=0, pattern=[[-1, P]], channel_multiplier=1).then_inc(ident_ok, 1)
            pool.memset(ones[:, :], 1.0).then_inc(consts, 1)
            pool.wait_ge(halves, 1)
            pool.wait_ge(var_eps_ok, 1)
            pool.tensor_tensor(rstd[:, 0:1], var_eps[:, 0:1], neg_half[:, 0:1], ALU.pow).then_inc(rstd_ok, 1)
            pool.wait_ge(wsim_in, 2 * 16)
            pool.wait_ge(consts, 1)
            pool.tensor_scalar(neg_w1[:, :], ones[:, :], wsim[:, 0:1], -1.0, ALU.mult, ALU.mult
                               ).then_inc(neg_w1_ok, 1)
            pool.tensor_scalar(neg_b[:, :], bsim[:, :], -1.0, None, ALU.mult).then_inc(neg_w1_ok, 1)
            pool.memset(earlier[:, :], 1.0).then_inc(consts, 1)
            pool.memset(ones_h[:, :], 1.0).then_inc(consts, 1)
            pool.wait_ge(var_eps_ok, 2)
            pool.tensor_tensor(rstd[:, 1:B], var_eps[:, 1:B], neg_half[:, 1:B], ALU.pow).then_inc(rstd_ok, 1)
            pool.memset(cx[:, :, :, D:D + 1], 1.0).then_inc(built, 1)
            pool.memset(tab0[:, :, :], 0.0).then_inc(consts, 1)
            pool.memset(rec[:, :, :], 0.0).then_inc(consts, 1)
            pool.memset(seen[:, 0, :], 0.0).then_inc(consts, 1)
            pool.iota(tab0_i[:, :], pattern=[[1, P]], base=SPARE, channel_multiplier=P).then_inc(consts, 1)
            pool.iota(trash_i[:, :], pattern=[[L, B * TOPK]], base=TRASH, channel_multiplier=1).then_inc(consts, 1)
            pool.iota(expert_i[:, :], pattern=[[1, E]], base=0, channel_multiplier=0).then_inc(consts, 1)
            pool.iota(rec_i[:, :, 0].rearrange("p (b k) -> p b k", k=TOPK), pattern=[[L, B], [0, TOPK]],
                      base=0, channel_multiplier=1).then_inc(consts, 1)
            pool.iota(rec_i[:, :, 1].rearrange("p (b k) -> p b k", k=TOPK), pattern=[[L * TOPK, B], [1, TOPK]],
                      base=0, channel_multiplier=TOPK).then_inc(consts, 1)
            pool.wait_ge(consts, 11)
            pool.tensor_copy(tab0[:, :, 1], tab0_i[:, :]).then_inc(filled, 1)
            pool.memset(zeros[:, :], 0.0).then_inc(zeroed, 1)
            pool.affine_select(out=earlier[:, :], in_=earlier[:, :], compare_op=ALU.is_gt, fill=0.0,
                               base=0, pattern=[[1, L]], channel_multiplier=-1).then_inc(built, 1)
            pool.tensor_copy(trash_row[:, :], trash_i[:, :]).then_inc(built, 1)
            pool.tensor_copy(expert_no[:, :], expert_i[:, :]).then_inc(built, 1)
            pool.tensor_copy(rec[:, :, 0:2], rec_i[:, :, :]).then_inc(built, 1)
            pool.wait_ge(const_in, 4 * 16)
            pool.wait_ge(x2_in, 16)
            pool.tensor_tensor(x2[:, :, :], x2[:, :, :],
                               bqv[:, :].unsqueeze(1).to_broadcast([L, B, D]), ALU.add).then_inc(x_bias, 1)
            pool.wait_ge(built, 5)

            def step(turn, r):
                s = STEP_RING * turn + r
                if there(s - 2):
                    pool.wait_ge(var_eps2_ok, s - 1)
                    pool.tensor_tensor(rstd2[:, :], var_eps2[:, :], neg_half[:, 0:1], ALU.pow).then_inc(rstd2_ok, 1)
                if there(s - 3):
                    b, k, next_k = s - 3, r % STEP_RING, (r + 1) % STEP_RING
                    pool.wait_ge(mask_ok, b + 1)
                    if past(s, 4):
                        pool.wait_ge(seen_ok, b)
                    pool.tensor_tensor(seen[:, next_k, :], seen[:, k, :], mask[:, :], ALU.add
                                       ).then_inc(seen_ok, 1)
                    if past(s, 6):
                        pool.wait_ge(rec_out[k], 16 * TOPK * (turn + (r - 3) // STEP_RING))
                    pool.tensor_copy(rec_now[:, k], rec[:, bass.ds(TOPK * b, TOPK), :]).then_inc(rec_now_ok, 1)
                    pool.wait_ge(table_init, 16)
                    pool.wait_ge(slot_ok, b + 1)
                    pool.wait_ge(gate_ok, b + 1)
                    for c in range(TOPK):
                        pool.indirect_dma_start(
                            out=table_d[:, :], out_offset=bass.IndirectOffsetOnAxis(ap=slot[:, k, c:c + 1], axis=0),
                            in_=rec_now[:, k, c, :], in_offset=None
                        ).then_inc(rec_out[k], 16)

            steps(pool, step)

            for k in range(STEP_RING):
                pool.wait_ge(rec_out[k], 16 * TOPK * len(range(k, B, STEP_RING)))
            pool.dma_start(tab0[:, :, :], table_d[0:E * CAP, :].rearrange("(j s) f -> j s f", s=P)
                           ).then_inc(table_in, 16)
            for k in range(STEP_RING):
                pool.wait_ge(xln_out[k], 16 * len(range(k, B, STEP_RING)))
            pool.wait_ge(table_ok, 3)
            pool.wait_ge(y_init, 16)

            def gather(j):
                pool.indirect_dma_start(
                    out=xg[:, j % G_RING, :], out_offset=None, in_=xln_d[:, :],
                    in_offset=bass.IndirectOffsetOnAxis(ap=token_ix[:, j:j + 1], axis=0)
                ).then_inc(gathered[j % G_RING], 16)

            for j in range(G_RING):
                gather(j)
            for j in range(NP):
                pool.wait_ge(yg_ok, j + 1)
                pool.indirect_dma_start(
                    out=y_d[:, :], out_offset=bass.IndirectOffsetOnAxis(ap=y_row[:, j:j + 1], axis=0),
                    in_=yg[:, j % Y_RING, :], in_offset=None).then_inc(y_out[j % Y_RING], 16)
                if j + G_RING < NP:
                    pool.wait_ge(xg_turned, j + 1)
                    gather(j + G_RING)

        @block.scalar
        def _(act):
            def step(turn, r):
                s = STEP_RING * turn + r
                if there(s - 1):
                    act.wait_ge(shifted_ok[GROUPS - 1], s)
                    if past(s, 2):
                        act.wait_ge(attn_ok, s - 1)
                    act.activation(probs[:, :], shifted[:, :], ACT.Exp).then_inc(probs_ok, 1)
                    act.wait_ge(neg_rmax_ok, s)
                    if past(s, 2):
                        act.wait_ge(enc_hc_ok, s - 1)
                    act.activation(batt[:, :], neg_r[:, :], ACT.Exp, bias=neg_rmax[:, :], scale=-1.0,
                                   accum_out=batt_sum[:, :]).then_inc(batt_ok, 1)
                if there(s - 2):
                    act.wait_ge(xln_turned, s - 1)
                    act.copy(xlnT[:, :], misc[:, 0:L]).then_inc(xlnT_ok, 1)
                if there(s - 1):
                    act.wait_ge(inv_ok, s)
                    act.activation(hq[:, :], attn_bank[0:L, 0:D], ACT.Copy, scale=inv_sum[:, :]
                                   ).then_inc(hq_ok, 1)
                if there(s + 1):
                    act.wait_ge(ctx_turned[0], s + 2)
                    act.copy(cxT[:, 0:REM + 3 * P], turnA[:, 0:REM + 3 * P]).then_inc(cxT_ok[0], 1)
                    act.wait_ge(enc_turned, s + 2)
                    if past(s, 2):
                        act.wait_ge(qv_ok, s - 1)
                    act.copy(encT[:, (r + 1) % STEP_RING, :], misc[:, 0:L]).then_inc(encT_ok, 1)
                    act.activation(query[:, :], misc[:, 0:L], ACT.Identity, scale=wsim[:, 2:3], bias=wsim[:, 1:2]
                                   ).then_inc(query_ok, 1)
                if there(s - 1):
                    act.wait_ge(hq_turned, s)
                    act.copy(hqT[:, :], attn_bank[:, 0:L]).then_inc(hqT_ok, 1)
                if there(s):
                    act.wait_ge(spread, s + 1)
                    if past(s, 1):
                        act.wait_ge(neg_r_ok, s)
                    act.copy(shift[:, :], max_bank[:, 0:2 * L]).then_inc(shift_ok, 1)
                if there(s + 1):
                    act.wait_ge(ctx_turned[1], s + 2)
                    act.copy(cxT[:, REM + 3 * P:REM + 7 * P], turnB[:, :]).then_inc(cxT_ok[1], 1)
                    act.wait_ge(ctx_turned[2], s + 2)
                    act.copy(cxT[:, REM + 7 * P:S], turnA[:, :]).then_inc(cxT_ok[2], 1)
                if there(s - 2):
                    act.wait_ge(top_d_ok, s - 1)
                    if past(s, 3):
                        act.wait_ge(gate_ok, s - 2)
                    act.activation(gate_e[:, :], top_d[:, :], ACT.Exp, accum_out=gate_sum[:, :]
                                   ).then_inc(gate_e_ok, 1)

            act.wait_ge(wsim_in, 2 * 16)
            steps(act, step)

            def ffn_step(turn, u):
                j = FFN_UNROLL * turn + u
                if there_pair(j):
                    act.wait_ge(down_ok, j + 1)
                    act.wait_ge(y_out[u % Y_RING], 16 * (turn + u // Y_RING))
                    act.activation(yg[:, u % Y_RING, :], down_bank[u % 2][:, 0:D], ACT.Copy,
                                   scale=gates[:, bass.ds(j, 1)]).then_inc(yg_ok, 1)
                if there_pair(j + 2):
                    act.wait_ge(biased, 2 * (j + 3))
                    act.activation(hidden[:, u % 2, :], hidden[:, u % 2, :], ACT.Gelu).then_inc(hidden_ok, 1)

            ffn_steps(act, ffn_step)

        @block.vector
        def _(dve):
            dve.memset(b2_rows[E:P, :], 0.0).then_inc(b2_padded, 1)
            def norm_x(b):
                dve.tensor_scalar(enc[:, :], xs[:, bass.ds(b, 1), :].rearrange("p o d -> p (o d)"),
                                  moments[:, bass.ds(b, 1), 0:1].rearrange("p o i -> p (o i)"),
                                  rstd[:, bass.ds(b, 1)], ALU.subtract, ALU.mult).then_inc(enc_ok, 1)

            dve.wait_ge(x0_in, 16)
            dve.bn_stats(stats[:, 0, :], xs[:, 0, :]).then_inc(stats_ok, 1)
            dve.wait_ge(stats_ok, 1)
            dve.bn_aggr(moments[:, 0, :], stats[:, 0, :]).then_inc(moments_ok, 1)
            dve.wait_ge(moments_ok, 1)
            dve.tensor_scalar(var_eps[:, 0:1], moments[:, 0, 1:2], EPS, None, ALU.add).then_inc(var_eps_ok, 1)
            dve.wait_ge(rstd_ok, 1)
            norm_x(0)
            dve.wait_ge(x_in, 16)
            for b in range(1, B):
                dve.bn_stats(stats[:, b, :], xs[:, b, :]).then_inc(stats_ok, 1)
            for b in range(1, B):
                dve.wait_ge(stats_ok, b + 1)
                dve.bn_aggr(moments[:, b, :], stats[:, b, :]).then_inc(moments_ok, 1)
            dve.wait_ge(moments_ok, B)
            dve.tensor_scalar(var_eps[:, 1:B], moments[:, 1:B, 1], EPS, None, ALU.add).then_inc(var_eps_ok, 1)
            dve.wait_ge(rstd_ok, 2)
            dve.wait_ge(neg_w1_ok, 2)

            def step(turn, r):
                s = STEP_RING * turn + r
                routed, chosen = there(s - 2), there(s - 3)
                if routed:
                    if not past(s, 3):
                        dve.wait_ge(x_bias, 1)
                        dve.wait_ge(built, 5)
                    row = x2[:, bass.ds(s - 2, 1), :].rearrange("p o d -> p (o d)")
                    dve.wait_ge(qv_ok, s - 1)
                    dve.tensor_tensor(row, misc[0:L, 0:D], row, ALU.add).then_inc(x2_ok, 1)
                if chosen:
                    b = s - 3
                    dve.wait_ge(top_ix_ok, b + 1)
                    dve.tensor_copy(top_no[:, :], top_ix[:, 0:TOPK]).then_inc(top_no_ok, 1)
                if routed:
                    if in_loop(s):
                        dve.wait_ge(built, 5)
                    dve.wait_ge(x2_ok, s - 1)
                    dve.bn_stats(st2[:, :], row).then_inc(st2_ok, 1)
                if chosen:
                    dve.wait_ge(top_no_ok, b + 1)
                    dve.tensor_scalar(pick0[:, :], expert_no[:, :], top_no[:, 0:1], None, ALU.is_equal
                                      ).then_inc(pick0_ok, 1)
                if routed:
                    if in_loop(s):
                        dve.wait_ge(built, 5)
                    dve.wait_ge(st2_ok, s - 1)
                    dve.bn_aggr(mv2[:, :], st2[:, :]).then_inc(mv2_ok, 1)
                if chosen:
                    dve.wait_ge(pick0_ok, b + 1)
                    dve.scalar_tensor_tensor(pick01[:, :], expert_no[:, :], top_no[:, 1:2], pick0[:, :],
                                             ALU.is_equal, ALU.add).then_inc(pick01_ok, 1)
                if routed:
                    dve.wait_ge(mv2_ok, s - 1)
                    dve.tensor_scalar(var_eps2[:, :], mv2[:, 1:2], EPS, None, ALU.add).then_inc(var_eps2_ok, 1)
                if chosen:
                    dve.wait_ge(pick01_ok, b + 1)
                    if past(s, 4):
                        dve.wait_ge(seen_ok, b)
                    dve.scalar_tensor_tensor(mask[:, :], expert_no[:, :], top_no[:, 2:3], pick01[:, :],
                                             ALU.is_equal, ALU.add).then_inc(mask_ok, 1)
                    dve.wait_ge(gate_e_ok, b + 1)
                    dve.reciprocal(gate_inv[:, :], gate_sum[:, :]).then_inc(gate_inv_ok, 1)
                if routed:
                    k = (r - 2) % STEP_RING
                    dve.wait_ge(rstd2_ok, s - 1)
                    if past(s, 5):
                        dve.wait_ge(xln_out[k], 16 * (turn + (r - 2) // STEP_RING))
                    dve.tensor_scalar(xln[:, k, :], x2[:, bass.ds(s - 2, 1), :].rearrange("p o d -> p (o d)"),
                                      mv2[:, 0:1], rstd2[:, :], ALU.subtract, ALU.mult).then_inc(xln_ok, 1)
                if there(s):
                    dve.wait_ge(sim_ok, s + 1)
                    if past(s, 1):
                        dve.wait_ge(max_turned, s)
                    dve.tensor_reduce(maxes[:, :],
                                      sim[:, :, 0:PER * L].rearrange("p g (t i) -> p i g t", t=PER),
                                      AX.XY, ALU.max).then_inc(maxes_ok, 1)
                if chosen:
                    dve.wait_ge(counted, b + 1)
                    for c in range(TOPK):
                        dve.scalar_tensor_tensor(pos_junk[:, c, :], expert_no[:, :], top_no[:, c:c + 1],
                                                 max_bank[0:L, 0:E], ALU.is_equal, ALU.mult,
                                                 accum_out=pos[:, c:c + 1]).then_inc(pos_ok, 1)
                if there(s - 1):
                    dve.wait_ge(batt_ok, s)
                    dve.tensor_tensor_reduce(hc_junk[:, :], batt[:, :], encT[:, (r - 1) % STEP_RING, :], 1.0, 0.0,
                                             ALU.mult, ALU.add, hc_raw[:, :]).then_inc(hc_raw_ok, 1)
                    dve.reciprocal(batt_inv[:, :], batt_sum[:, :]).then_inc(batt_inv_ok, 1)
                if chosen:
                    dve.wait_ge(pos_ok, TOPK * (b + 1))
                    dve.scalar_tensor_tensor(slot_b[:, :], top_no[:, :], float(CAP), pos[:, :],
                                             ALU.mult, ALU.add).then_inc(slot_b_ok, 1)
                    dve.scalar_tensor_tensor(over[:, :], pos[:, :], float(CAP),
                                             trash_row[:, bass.ds(TOPK * b, TOPK)],
                                             ALU.is_ge, ALU.mult).then_inc(over_ok, 1)
                if there(s - 1):
                    dve.wait_ge(hc_raw_ok, s)
                    dve.wait_ge(batt_inv_ok, s)
                    dve.tensor_scalar(enc_hc[:, :], encT[:, (r - 1) % STEP_RING, :], hc_raw[:, :], batt_inv[:, :],
                                      ALU.mult, ALU.mult).then_inc(enc_hc_ok, 1)
                if chosen:
                    dve.wait_ge(gate_inv_ok, b + 1)
                    dve.wait_ge(rec_now_ok, b + 1)
                    dve.tensor_scalar(rec_now[:, r % STEP_RING, :, 2], gate_e[:, :], gate_inv[:, :], None,
                                      ALU.mult).then_inc(gate_ok, 1)
                    dve.wait_ge(slot_b_ok, b + 1)
                    dve.wait_ge(over_ok, b + 1)
                    if past(s, 6):
                        dve.wait_ge(rec_out[r % STEP_RING], 16 * TOPK * (turn + (r - 3) // STEP_RING))
                    dve.tensor_tensor(slot[:, r % STEP_RING, :], slot_b[:, :], over[:, :], ALU.max
                                      ).then_inc(slot_ok, 1)
                if there(s - 1):
                    dve.wait_ge(attn_ok, s)
                    if past(s, 2):
                        dve.wait_ge(hq_ok, s - 1)
                    dve.reciprocal(inv_sum[:, :], attn_bank[0:L, D:D + 1]).then_inc(inv_ok, 1)
                if there(s):
                    dve.wait_ge(max_turned, s + 1)
                    dve.tensor_reduce(row_max[:, :], max_bank[0:L, 0:P], AX.X, ALU.max).then_inc(row_max_ok, 1)
                if routed:
                    dve.wait_ge(logits_raw, s - 1)
                    dve.tensor_tensor(logits[:, :], misc[0:L, 0:E], gateb[:, :], ALU.add).then_inc(logits_ok, 1)
                if there(s):
                    dve.wait_ge(row_max_ok, s + 1)
                    dve.tensor_scalar(neg_diag[:, :], ident[0:L, 0:L], row_max[:, :], -1.0, ALU.mult, ALU.mult
                                      ).then_inc(diag_ok, 1)
                if routed:
                    if in_loop(s):
                        dve.wait_ge(built, 5)
                    dve.wait_ge(logits_ok, s - 1)
                    dve.max(top[:, :], logits[:, :]).then_inc(top_ok, 1)
                    if in_loop(s):
                        dve.wait_ge(built, 5)
                    dve.wait_ge(top_ok, s - 1)
                    dve.max_index(top_ix[:, :], top[:, :], logits[:, :]).then_inc(top_ix_ok, 1)
                    if past(s, 3):
                        dve.wait_ge(gate_e_ok, s - 2)
                    dve.tensor_scalar(top_d[:, :], top[:, 0:TOPK], top[:, 0:1], None, ALU.subtract
                                      ).then_inc(top_d_ok, 1)
                if there(s - 1):
                    dve.wait_ge(hqT_ok, s)
                    dve.tensor_tensor(enc_hq[:, :], encT[:, (r - 1) % STEP_RING, :], hqT[:, :], ALU.mult
                                      ).then_inc(enc_hq_ok, 1)
                if there(s):
                    dve.wait_ge(shift_ok, s + 1)
                    if past(s, 1):
                        dve.wait_ge(probs_ok, s)
                    for g in range(GROUPS):
                        w = PER * L
                        dve.tensor_tensor(shifted[:, g * w:(g + 1) * w].rearrange("p (t i) -> p t i", t=PER),
                                          sim[:, g, 0:w].rearrange("p (t i) -> p t i", t=PER),
                                          shift[:, 0:L].unsqueeze(1).to_broadcast([P, PER, L]),
                                          ALU.add).then_inc(shifted_ok[g], 1)
                    if past(s, 1):
                        dve.wait_ge(batt_ok, s)
                    dve.scalar_tensor_tensor(neg_r[:, :], shift[:, 0:L], neg_b[:, :], shift[:, L:2 * L],
                                             ALU.add, ALU.add).then_inc(neg_r_ok, 1)
                if there(s + 2):
                    dve.wait_ge(enc_turned, s + 2)
                    norm_x(s + 2)
                if there(s):
                    dve.wait_ge(neg_r_ok, s + 1)
                    dve.tensor_reduce(neg_rmax[:, :], neg_r[:, :], AX.X, ALU.min).then_inc(neg_rmax_ok, 1)

            steps(dve, step)

            dve.wait_ge(b_turned, 1)
            dve.tensor_copy(b1T[:, :].rearrange("p (e c) -> p c e", c=HC),
                            sim[:, 0, 0:HC * E].rearrange("p (c e) -> p c e", c=HC)).then_inc(b_kept, 1)
            dve.wait_ge(table_turned, 1)
            dve.tensor_copy(token_ix[:, :], sim[:, 1, 0:NP]).then_inc(table_ok, 1)
            dve.tensor_copy(y_row[:, :], sim[:, 1, NP:2 * NP]).then_inc(table_ok, 1)
            dve.tensor_copy(gates[:, :], sim[:, 1, 2 * NP:3 * NP]).then_inc(table_ok, 1)
            dve.wait_ge(b_kept, 1)

            def ffn_step(turn, u):
                j = FFN_UNROLL * turn + u
                if there_pair(j + 3):
                    dve.wait_ge(xg_turned, j + 4)
                    if not isinstance(j, int) or j >= -1:
                        dve.wait_ge(up_ok, j + 2)
                    dve.tensor_copy(xgT[:, (u + 3) % 2, :], xg_bank[(u + 3) % 2][:, 0:P]).then_inc(xgT_ok, 1)
                if there_pair(j + 2):
                    dve.wait_ge(up_ok, j + 3)
                    for e in range(2):
                        own = slice(e * CAP, (e + 1) * CAP)
                        dve.tensor_tensor(hidden[:, u % 2, e * HC * CAP:(e + 1) * HC * CAP]
                                          .rearrange("p (c s) -> p c s", s=CAP),
                                          up_bank[u % 2][e].rearrange("p (c s) -> p c s", s=P)[:, :, own],
                                          b1T[:, bass.ds(2 * HC * (j + 2) + HC * e, HC)].unsqueeze(2)
                                          .to_broadcast([P, HC, CAP]), ALU.add).then_inc(biased, 1)

            ffn_steps(dve, ffn_step)

            for c in range(4):
                dve.wait_ge(y_in[c], 32)
                mine = x2[:, 4 * c:4 * c + 4, :]
                for k in range(TOPK):
                    if k:
                        dve.wait_ge(sum_part, 2 * c + k)
                    dve.tensor_tensor(mine, mine, yk[:, 4 * c:4 * c + 4, k * D:(k + 1) * D], ALU.add
                                      ).then_inc(sum_part if k < TOPK - 1 else sum_ok, 1)

        @block.tensor
        def _(pe):
            def turn_tiles(target, first, slots, k):
                for i in slots:
                    n = rows_of(i)
                    at = tile_cols(i).start - first
                    last = pe.transpose(target[:, at:at + n], cx[0:n, k, i, 0:D], ident[0:n, 0:n])
                return last

            def step(turn, r):
                s = STEP_RING * turn + r
                old, now, new = (r - 1) % STEP_RING, r % STEP_RING, (r + 1) % STEP_RING
                if there(s):
                    pe.wait_ge(query_ok, s + 1)
                    for g in range(GROUPS):
                        pe.wait_ge(cxT_ok[g], s + 1)
                        if past(s, 1):
                            pe.wait_ge(shifted_ok[g], s)
                        for t in range(PER):
                            last = pe.matmul(sim[:, g, t * L:(t + 1) * L], cxT[:, tile_cols(g * PER + t)],
                                             query[:, :], start=True, stop=True)
                    last.then_inc(sim_ok, 1)
                if there(s - 3):
                    b = s - 3
                    pe.wait_ge(mask_ok, b + 1)
                    if past(s, 4):
                        pe.wait_ge(seen_ok, b)
                    if there(s - 1):
                        pe.wait_ge(shift_ok, s)
                    else:
                        pe.wait_ge(pos_ok, TOPK * b)
                    pe.matmul(max_bank[0:L, 0:E], earlier[:, :], mask[:, :], start=True, stop=False)
                    pe.matmul(max_bank[0:L, 0:E], ones_h[:, :], seen[:, now, :],
                              start=False, stop=True).then_inc(counted, 1)
                if there(s - 2):
                    pe.wait_ge(xln_ok, s - 1)
                    pe.transpose(misc[:, 0:L], xln[:, (r - 2) % STEP_RING, :], ident[0:L, 0:L]
                                 ).then_inc(xln_turned, 1)
                if there(s - 1):
                    pe.wait_ge(probs_ok, s)
                    if past(s, 2):
                        pe.wait_ge(hqT_ok, s - 1)
                    else:
                        pe.wait_ge(built, 5)
                    for i in range(TILES):
                        n = rows_of(i)
                        last = pe.matmul(attn_bank[0:L, 0:D + 1], probs[0:n, i * L:(i + 1) * L],
                                         cx[0:n, old, i, :], start=(i == 0), stop=(i == TILES - 1))
                    last.then_inc(attn_ok, 1)
                if there(s - 2):
                    pe.wait_ge(xlnT_ok, s - 1)
                    if not past(s, 3):
                        pe.wait_ge(const_in, 4 * 16)
                    pe.matmul(misc[0:L, 0:E], xlnT[:, :], gatew[:, :], start=True, stop=True
                              ).then_inc(logits_raw, 1)
                if there(s):
                    pe.wait_ge(maxes_ok, s + 1)
                    if there(s - 3):
                        pe.wait_ge(pos_ok, TOPK * (s - 2))
                    elif past(s, 1):
                        pe.wait_ge(shift_ok, s)
                    pe.transpose(max_bank[0:L, 0:P], maxes[:, :], ident[:, :]).then_inc(max_turned, 1)
                if there(s + 1):
                    pe.wait_ge(ctx_in[new], 32 * (turn + (r + 1) // STEP_RING + 1))
                    if past(s, 0):
                        pe.wait_ge(cxT_ok[2], s + 1)
                    turn_tiles(turnA, 0, (1, 2, 3, 0), new).then_inc(ctx_turned[0], 1)
                    if past(s, 0):
                        pe.wait_ge(cxT_ok[1], s + 1)
                    turn_tiles(turnB, REM + 3 * P, range(PER, 2 * PER), new).then_inc(ctx_turned[1], 1)
                    pe.wait_ge(enc_ok, s + 2)
                    if there(s - 2):
                        pe.wait_ge(logits_ok, s - 1)
                    pe.transpose(misc[:, 0:L], enc[:, :], ident[0:L, 0:L]).then_inc(enc_turned, 1)
                if there(s - 1):
                    pe.wait_ge(hq_ok, s)
                    pe.transpose(attn_bank[:, 0:L], hq[:, :], ident[0:L, 0:L]).then_inc(hq_turned, 1)
                if there(s):
                    pe.wait_ge(diag_ok, s + 1)
                    pe.matmul(max_bank[:, 0:L], ones[0:L, :], neg_diag[:, :], start=True, stop=True)
                    pe.matmul(max_bank[:, L:2 * L], neg_w1[:, :], encT[:, now, :], start=True, stop=True
                              ).then_inc(spread, 1)
                if there(s + 1):
                    pe.wait_ge(cxT_ok[0], s + 2)
                    turn_tiles(turnA, REM + 7 * P, range(2 * PER, TILES), new).then_inc(ctx_turned[2], 1)
                if there(s - 1):
                    if there(s + 1):
                        pe.wait_ge(query_ok, s + 2)
                    else:
                        pe.wait_ge(logits_ok, s - 1)
                    if not past(s, 2):
                        pe.wait_ge(const_in, 4 * 16)
                    pe.matmul(misc[0:L, 0:D], encT[:, old, :], wqv[:, 0, :], start=True, stop=False)
                    pe.wait_ge(enc_hc_ok, s)
                    pe.matmul(misc[0:L, 0:D], enc_hc[:, :], wqv[:, 3, :], start=False, stop=False)
                    pe.wait_ge(hqT_ok, s)
                    pe.matmul(misc[0:L, 0:D], hqT[:, :], wqv[:, 1, :], start=False, stop=False)
                    pe.wait_ge(enc_hq_ok, s)
                    pe.matmul(misc[0:L, 0:D], enc_hq[:, :], wqv[:, 2, :], start=False, stop=True
                              ).then_inc(qv_ok, 1)

            pe.wait_ge(ident_ok, 1)
            pe.wait_ge(neg_w1_ok, 2)
            steps(pe, step)

            pe.wait_ge(bias_in, 32)
            pe.wait_ge(b2_padded, 1)
            for c in range(HC):
                last = pe.transpose(sim[:, 0, c * E:(c + 1) * E],
                                    b1_rows[:, :].rearrange("e (p c) -> e c p", c=HC)[:, c, :], ident[0:E, 0:E])
            last.then_inc(b_turned, 1)
            pe.wait_ge(table_in, 16)
            for f in range(3):
                last = pe.transpose(sim[:, 1, f * NP:(f + 1) * NP], tab0[:, :, f], ident[0:NP, 0:NP])
            last.then_inc(table_turned, 1)
            pe.wait_ge(b_kept, 1)
            pe.wait_ge(table_ok, 3)

            def turn_tokens(turn, u):
                j = W_RING * turn + u
                pe.wait_ge(gathered[u % G_RING], 16 * (W_RING // G_RING * turn + u // G_RING + 1))
                if not isinstance(j, int) or j >= 2:
                    pe.wait_ge(xgT_ok, j - 1)
                pe.transpose(xg_bank[u % 2][:, 0:P], xg[:, u % G_RING, :], ident[:, :]).then_inc(xg_turned, 1)

            def up(turn, u):
                j = W_RING * turn + u
                k = u % W_RING
                pe.wait_ge(w_next[k], 32 * (turn + u // W_RING))
                pe.wait_ge(xgT_ok, j + 1)
                if not isinstance(j, int) or j >= 2:
                    pe.wait_ge(biased, 2 * (j - 1))
                for e in range(2):
                    w = wring[:, k, 0, e].rearrange("p (m c) -> p c m", c=HC)
                    for c in range(HC):
                        last = pe.matmul(up_bank[u % 2][e][:, c * P:(c + 1) * P], w[:, c, :],
                                         xgT[:, u % 2, :], start=True, stop=True)
                last.then_inc(up_ok, 1)

            def down(turn, u):
                j = W_RING * turn + u
                k = u % W_RING
                pe.wait_ge(hidden_ok, j + 1)
                if not isinstance(j, int) or j >= 2:
                    pe.wait_ge(yg_ok, j - 1)
                for c in range(-1, HC):
                    for e in range(2):
                        at = (e * HC + c) * CAP
                        if c < 0:
                            chooser = ident[:, 2 * j + e:2 * j + e + 1].to_broadcast([P, CAP])
                            weights = b2_rows[:, :]
                        else:
                            chooser = hidden[:, u % 2, at:at + CAP]
                            weights = wring[:, k, 1, e, c * D:(c + 1) * D]
                        last = pe.matmul(down_bank[u % 2][e * CAP:(e + 1) * CAP, 0:D], chooser, weights,
                                         start=(c < 0), stop=(c == HC - 1))
                last.then_inc(down_ok, 1)

            pe.wait_ge(w_first, 32 * W_RING)
            turn_tokens(0, 0)
            turn_tokens(0, 1)
            up(0, 0)
            turn_tokens(0, 2)
            up(0, 1)

            def ffn_step(turn, u, more):
                down(turn, u)
                if more > 2:
                    turn_tokens(turn, u + 3)
                if more > 1:
                    up(turn, u + 2)

            for turn in range(NP // W_RING):
                for u in range(W_RING):
                    ffn_step(turn, u, NP - 1 - (W_RING * turn + u))


_INS = ['x', 'ctx_1024', 'L0_xattn_w_sim', 'L0_xattn_b_sim', 'L0_xattn_W_qv', 'L0_xattn_b_qv', 'L0_ffn_gate_w',
        'L0_ffn_gate_b', 'L0_ffn_w1', 'L0_ffn_b1', 'L0_ffn_w2', 'L0_ffn_b2']


def kernel(**inputs):
    import numpy as np
    import concourse.bacc as bacc
    from concourse.bass_utils import run_bass_kernel_spmd

    nc = bacc.Bacc("TRN2", target_bir_lowering=False, num_devices=1)
    arrays, args = {}, []
    for name in _INS:
        a = np.ascontiguousarray(inputs[name])
        arrays[f"in_{name}"] = a
        args.append(nc.dram_tensor(f"in_{name}", a.shape, mybir.dt.from_np(a.dtype), kind="ExternalInput").ap())
    shape = inputs['x'].shape
    args.append(nc.dram_tensor("out_0", shape, F32, kind="ExternalOutput").ap())
    build_xattn_moe(nc, *args)
    result = run_bass_kernel_spmd(nc, [arrays], core_ids=[0])
    return result.results[0]["out_0"]
```

```python
from contextlib import ExitStack

import concourse.bass as bass
from concourse import mybir

ALU = mybir.AluOpType
ACT = mybir.ActivationFunctionType
AX = mybir.AxisListType
F32 = mybir.dt.float32
BF16 = mybir.dt.bfloat16
I32 = mybir.dt.int32
U32 = mybir.dt.uint32

P = 128
TOPK = 3
CAP = 64
EPS = 1e-5
BANK = 512
STEP_RING = 3
W_RING = 16
G_RING = 8
Y_RING = 4
HEAD = 2
ROW_FILLS = 2
Y_FILLS = 4
OUT_PARTS = 8
POOL_PARTS = (3, 6)
FFN_UNROLL = 8


def build_xattn_moe(nc, x, ctx, w_sim, b_sim, w_qv, b_qv, gate_w, gate_b, w1, b1, w2, b2, out):
    B, L, D = x.shape
    S = ctx.shape[1]
    E, _, H = w1.shape
    T = B * L
    MAIN = S // P
    REM = S - MAIN * P
    TILES = MAIN + 1
    GROUPS = 3
    PER = TILES // GROUPS
    NP = E // 2
    HC = H // P
    TRASH = (E - 1) * CAP + T
    W = D + 2
    SPARE = T * TOPK
    assert D == P and TILES == GROUPS * PER and NP == 2 * W_RING and 2 * CAP == P

    slots_d = nc.dram_tensor("slots_scratch", (TRASH + T * TOPK, W), F32)
    y_d = nc.dram_tensor("y_scratch", (SPARE + E * CAP, D), F32)

    with ExitStack() as stack:
        def sb(name, shape, dt=F32):
            return stack.enter_context(nc.sbuf_tensor(name, shape, dt))

        def sem(name):
            return stack.enter_context(nc.semaphore(name))

        def sems(name, n):
            return [sem(f"{name}{i}") for i in range(n)]

        ident = sb("ident", [P, P])
        ones = sb("ones", [P, P])
        earlier = sb("earlier", [L, L], BF16)
        ones_h = sb("ones_h", [L, L], BF16)
        expert_no = sb("expert_no", [L, E])
        expert_i = sb("expert_i", [L, E], I32)
        trash_row = sb("trash_row", [L, B * TOPK])
        trash_i = sb("trash_i", [L, B * TOPK], I32)
        neg_half = sb("neg_half", [L, B])
        table_junk = sb("table_junk", [L, 1])
        wsim = sb("wsim", [P, 3])
        neg_w1 = sb("neg_w1", [P, P])
        neg_b = sb("neg_b", [P, 1])
        bsim = sb("bsim", [P, 1])
        wqv = sb("wqv", [P, 4, D])
        bqv = sb("bqv", [L, D])
        gatew = sb("gatew", [P, E])
        gateb = sb("gateb", [L, E])
        b1_rows = sb("b1_rows", [E, H])
        b1T = sb("b1T", [P, E * HC])
        b2_rows = sb("b2_rows", [P, D])
        xs = sb("xs", [L, B, D])
        x2 = sb("x2", [L, B, D])
        stats = sb("stats", [L, B, 6])
        moments = sb("moments", [L, B, 2])
        var_eps = sb("var_eps", [L, B])
        rstd = sb("rstd", [L, B])
        lower = sb("lower", [L, B])
        rows = sb("rows", [L, STEP_RING, TOPK, W])
        y_no = sb("y_no", [L, B * TOPK])
        y_no_i = sb("y_no_i", [L, B * TOPK], I32)
        cx = sb("cx", [P, STEP_RING, TILES, D + 1])
        cxT = sb("cxT", [P, S])
        enc = sb("enc", [L, D])
        encT = sb("encT", [P, STEP_RING, L])
        query = sb("query", [P, L])
        maxes = sb("maxes", [P, L])
        row_max = sb("row_max", [L, 1])
        neg_diag = sb("neg_diag", [L, L])
        shift = sb("shift", [P, 2 * L])
        shifted = sb("shifted", [P, TILES * L])
        probs = sb("probs", [P, TILES * L])
        inv_sum = sb("inv_sum", [L, 1])
        hq = sb("hq", [L, D])
        hqT = sb("hqT", [P, L])
        enc_hq = sb("enc_hq", [P, L])
        neg_r = sb("neg_r", [P, L])
        neg_rmax = sb("neg_rmax", [P, 1])
        batt = sb("batt", [P, L])
        batt_sum = sb("batt_sum", [P, 1])
        hc_junk = sb("hc_junk", [P, L])
        hc_raw = sb("hc_raw", [P, 1])
        hc_bar = sb("hc_bar", [P, 1])
        batt_inv = sb("batt_inv", [P, 1])
        enc_hc = sb("enc_hc", [P, L])
        st2 = sb("st2", [L, 6])
        mv2 = sb("mv2", [L, 2])
        var_eps2 = sb("var_eps2", [L, 1])
        rstd2 = sb("rstd2", [L, 1])
        xlnT = sb("xlnT", [P, L])
        logits = sb("logits", [L, E])
        top = sb("top", [L, 8])
        top_ix = sb("top_ix", [L, 8], U32)
        top_no = sb("top_no", [L, TOPK])
        pick0 = sb("pick0", [L, E])
        pick01 = sb("pick01", [L, E])
        mask = sb("mask", [L, E], BF16)
        seen = sb("seen", [L, STEP_RING, E], BF16)
        pos_junk = sb("pos_junk", [L, TOPK, E])
        pos = sb("pos", [L, TOPK])
        top_d = sb("top_d", [L, TOPK])
        gate_e = sb("gate_e", [L, TOPK])
        gate_sum = sb("gate_sum", [L, 1])
        gate_inv = sb("gate_inv", [L, 1])
        slot_b = sb("slot_b", [L, TOPK])
        over = sb("over", [L, TOPK])
        slot = sb("slot", [L, STEP_RING, TOPK], I32)
        chooser = sb("chooser", [P, 2, P])
        y_ix = sb("y_ix", [P, NP], I32)
        spare_i = sb("spare_i", [P, NP], I32)
        wring = sb("wring", [P, W_RING, 2, 2, HC * D])
        spent = cx[:, :, :, :].rearrange("p k t d -> p (k t d)")

        def reuse(first, count, width):
            return spent[:, first:first + count * width].rearrange("p (n w) -> p n w", n=count)

        xg = reuse(0, G_RING, W)
        xgT = reuse(G_RING * W, 2, P)
        yg = reuse(G_RING * W + 2 * P, Y_RING, D)
        hidden = shifted[:, 0:2 * H].rearrange("p (n w) -> p n w", n=2)
        hiddenT = probs[:, 0:2 * H].rearrange("p (n w) -> p n w", n=2)
        zeros = sb("zeros", [P, 400])
        blank = wring[:, W_RING - 3:W_RING].rearrange("p s a e n -> p (s a e n)")[:, 0:NP * W].rearrange(
            "p (j w) -> p j w", w=W)
        yk = wring[0:L, 0:3].rearrange("p s a e n -> p (s a e n)").rearrange("p (b n) -> p b n", b=B)

        bank = [stack.enter_context(nc.psum_tensor(f"bank{i}", [P, BANK], F32)) for i in range(3, 8)]
        sim = stack.enter_context(nc.psum_tensor("sim", [P, GROUPS, BANK], F32))
        turnA, turnB, attn_bank, max_bank, misc = bank

        const_in = sem("const_in")
        wsim_in = sem("wsim_in")
        x0_in = sem("x0_in")
        x_in = sem("x_in")
        ident_ok = sem("ident_ok")
        cleared = sem("cleared")
        x2_in = sem("x2_in")
        bias_in = sem("bias_in")
        b_turned = sem("b_turned")
        b_kept = sem("b_kept")
        b2_padded = sem("b2_padded")
        ctx_in = sems("ctx_in", STEP_RING)
        w_first = sem("w_first")
        w_next = sems("w_next", W_RING)
        filled = sem("filled")
        zeroed = sem("zeroed")
        rows_init = sem("rows_init")
        blanked = sem("blanked")
        y_init = sem("y_init")
        consts = sem("consts")
        halves = sem("halves")
        table_there = sem("table_there")
        built = sem("built")
        neg_w1_ok = sem("neg_w1_ok")
        x_bias = sem("x_bias")
        stats_ok = sem("stats_ok")
        moments_ok = sem("moments_ok")
        rstd_ok = sem("rstd_ok")
        lower_ok = sem("lower_ok")
        hc_ok = sem("hc_ok")
        enc_ok = sem("enc_ok")
        enc_turned = sem("enc_turned")
        encT_ok = sem("encT_ok")
        query_ok = sem("query_ok")
        ctx_turned = sems("ctx_turned", GROUPS)
        cxT_ok = sems("cxT_ok", GROUPS)
        sim_ok = sem("sim_ok")
        maxes_ok = sem("maxes_ok")
        max_turned = sem("max_turned")
        row_max_ok = sem("row_max_ok")
        diag_ok = sem("diag_ok")
        spread = sem("spread")
        shift_ok = sem("shift_ok")
        shifted_ok = sems("shifted_ok", GROUPS)
        probs_ok = sem("probs_ok")
        attn_ok = sem("attn_ok")
        inv_ok = sem("inv_ok")
        hq_ok = sem("hq_ok")
        hq_turned = sem("hq_turned")
        hqT_ok = sem("hqT_ok")
        enc_hq_ok = sem("enc_hq_ok")
        neg_r_ok = sem("neg_r_ok")
        neg_rmax_ok = sem("neg_rmax_ok")
        batt_ok = sem("batt_ok")
        hc_raw_ok = sem("hc_raw_ok")
        batt_inv_ok = sem("batt_inv_ok")
        enc_hc_ok = sem("enc_hc_ok")
        qv_ok = sem("qv_ok")
        x2_ok = sem("x2_ok")
        st2_ok = sem("st2_ok")
        mv2_ok = sem("mv2_ok")
        var_eps_ok = sem("var_eps_ok")
        var_eps2_ok = sem("var_eps2_ok")
        rstd2_ok = sem("rstd2_ok")
        xln_ok = sem("xln_ok")
        rows_ok = sem("rows_ok")
        xln_turned = sem("xln_turned")
        xlnT_ok = sem("xlnT_ok")
        logits_raw = sem("logits_raw")
        logits_ok = sem("logits_ok")
        top_ok = sem("top_ok")
        top_ix_ok = sem("top_ix_ok")
        top_no_ok = sem("top_no_ok")
        pick0_ok = sem("pick0_ok")
        pick01_ok = sem("pick01_ok")
        mask_ok = sem("mask_ok")
        seen_ok = sem("seen_ok")
        counted = sem("counted")
        pos_ok = sem("pos_ok")
        top_d_ok = sem("top_d_ok")
        gate_e_ok = sem("gate_e_ok")
        gate_inv_ok = sem("gate_inv_ok")
        gate_ok = sem("gate_ok")
        slot_b_ok = sem("slot_b_ok")
        over_ok = sem("over_ok")
        slot_ok = sem("slot_ok")
        y_no_ok = sem("y_no_ok")
        rec_out = sems("rec_out", STEP_RING)
        tokens_in = sems("tokens_in", G_RING)
        y_ix_ok = sem("y_ix_ok")
        chooser_ok = sem("chooser_ok")
        xg_turned = sem("xg_turned")
        xgT_ok = sem("xgT_ok")
        up_ok = sem("up_ok")
        biased = sem("biased")
        hidden_turned = sem("hidden_turned")
        up_kept = sem("up_kept")
        hidden_ok = sem("hidden_ok")
        down_ok = sem("down_ok")
        yg_ok = sem("yg_ok")
        y_out = sems("y_out", Y_RING)
        y_in = sems("y_in", OUT_PARTS)
        vector_part = sem("vector_part")
        vector_sum = sem("vector_sum")
        pool_part = sem("pool_part")
        pool_sum = sem("pool_sum")
        out_sem = sem("out_sem")

        LAST_STEP = B + 2
        PEEL = 3 + STEP_RING
        LOOPS = (B - 2 - PEEL) // STEP_RING
        TAIL = range(PEEL + LOOPS * STEP_RING, LAST_STEP + 1)

        def there(b):
            return not isinstance(b, int) or 0 <= b < B

        def past(s, n):
            return not isinstance(s, int) or s >= n

        def in_loop(s):
            return not isinstance(s, int)

        def steps(eng, step):
            for r in range(-1, PEEL):
                step(0, r)
            with eng.Fori(1, 1 + LOOPS) as turn:
                for r in range(PEEL - STEP_RING, PEEL):
                    step(turn, r)
            for s in TAIL:
                step(0, s)

        def there_pair(j):
            return not isinstance(j, int) or 0 <= j < NP

        def ffn_steps(eng, step):
            for u in range(-4, FFN_UNROLL):
                step(0, u)
            with eng.Fori(1, NP // FFN_UNROLL - 1) as turn:
                for u in range(FFN_UNROLL):
                    step(turn, u)
            for j in range(NP - FFN_UNROLL, NP):
                step(0, j)

        up_bank = [sim[:, 0], sim[:, 1]]
        hT_bank = [sim[:, 2], turnA[:, :]]
        down_bank = [turnB, attn_bank]
        xg_bank = [max_bank, misc]

        def tile_cols(slot_no):
            start = 0 if slot_no == 0 else REM + (slot_no - 1) * P
            return slice(start, start + P)

        def rows_of(slot_no):
            return REM if slot_no == 0 else P

        def sum_parts(eng, parts, part, done):
            per = B // OUT_PARTS
            for n, c in enumerate(parts):
                mine = x2[:, c * per:(c + 1) * per, :]
                y0, y1, y2 = (yk[:, c * per:(c + 1) * per, k * D:(k + 1) * D] for k in range(TOPK))
                eng.wait_ge(y_in[c], 16)
                eng.tensor_tensor(y0, y0, y1, ALU.add).then_inc(part, 1)
                eng.tensor_tensor(mine, mine, y2, ALU.add).then_inc(part, 1)
                eng.wait_ge(part, 2 * (n + 1))
                eng.tensor_tensor(mine, mine, y0, ALU.add).then_inc(done, 1)

        block = stack.enter_context(nc.Block())

        @block.sync
        def _(sp):
            def load_ctx(turn, r):
                k = r % STEP_RING
                b = STEP_RING * turn + r
                sp.dma_start(cx[:, k, 1:TILES, 0:D],
                             ctx[bass.ds(b, 1), 0:MAIN * P, :].rearrange("o (p t) d -> p (o t) d", t=MAIN)
                             ).then_inc(ctx_in[k], 16)
                sp.dma_start(cx[0:REM, k, 0, 0:D],
                             ctx[bass.ds(b, 1), MAIN * P:S, :].rearrange("o p d -> p (o d)")
                             ).then_inc(ctx_in[k], 16)

            def load_weights(pair, k, done):
                sp.dma_start(wring[:, bass.ds(k, 1), 0].rearrange("p o e n -> p (o e) n"),
                             w1[bass.ds(2 * pair, 2)].rearrange("e d h -> d e h")).then_inc(done, 16)
                sp.dma_start(wring[:, bass.ds(k, 1), 1].rearrange("p o e n -> p (o e) n"),
                             w2[bass.ds(2 * pair, 2)].rearrange("e (p c) n -> p e (c n)", c=HC)
                             ).then_inc(done, 16)

            sp.dma_start(xs[:, 0:HEAD, :], x[0:HEAD].rearrange("b l d -> l b d")).then_inc(x0_in, 16)
            load_ctx(0, 0)
            sp.dma_start(wsim[:, :], w_sim.rearrange("(c d) -> d c", d=D), allow_slow_non_contiguous=True
                         ).then_inc(wsim_in, 16)
            sp.dma_start(bsim[:, :], b_sim.partition_broadcast(P)).then_inc(wsim_in, 16)
            sp.dma_start(xs[:, HEAD:B, :], x[HEAD:B].rearrange("b l d -> l b d")).then_inc(x_in, 16)
            load_ctx(0, 1)
            sp.dma_start(bqv[:, :], b_qv.partition_broadcast(L)).then_inc(const_in, 16)
            sp.dma_start(wqv[:, :, :], w_qv.rearrange("(c d) n -> d c n", d=D)).then_inc(const_in, 16)
            sp.dma_start(x2[:, :, :], x.rearrange("b l d -> l b d")).then_inc(x2_in, 16)
            sp.dma_start(gatew[:, :], gate_w).then_inc(const_in, 16)
            sp.dma_start(gateb[:, :], gate_b.partition_broadcast(L)).then_inc(const_in, 16)
            sp.dma_start(b1_rows[:, :], b1).then_inc(bias_in, 16)
            sp.dma_start(b2_rows[0:E, :], b2).then_inc(bias_in, 16)
            load_weights(0, 0, w_first)

            y_blocks = SPARE * D // P // 400

            def step(turn, r):
                s = STEP_RING * turn + r
                if there(s + 2):
                    if past(s, 1):
                        sp.wait_ge(attn_ok, s)
                    if past(s, 0):
                        load_ctx(turn, r + 2)
                    load_weights(s + 2, s + 2, w_first)
                if not past(s, ROW_FILLS) and s >= 0:
                    first, behind = s * NP // ROW_FILLS, (s + 1) * NP // ROW_FILLS
                    sp.wait_ge(filled, 1)
                    sp.dma_start(slots_d[first * P:behind * P, :].rearrange("(j s) w -> s j w", s=P),
                                 blank[:, first:behind, :]).then_inc(rows_init, 16)
                if not past(s, ROW_FILLS + Y_FILLS) and s >= ROW_FILLS:
                    part = s - ROW_FILLS
                    first, behind = part * y_blocks // Y_FILLS, (part + 1) * y_blocks // Y_FILLS
                    sp.wait_ge(zeroed, 1)
                    sp.dma_start(y_d[0:SPARE, :].rearrange("r d -> (r d)")
                                 .rearrange("(p n w) -> p n w", p=P, w=400)[:, first:behind],
                                 zeros[:, :].unsqueeze(1).to_broadcast([P, behind - first, 400])
                                 ).then_inc(y_init, 16)
                if isinstance(s, int) and s == PEEL - 1:
                    sp.wait_ge(rows_init, 16 * ROW_FILLS)

            steps(sp, step)

            def load_tokens(j):
                sp.dma_start(xg[:, j % G_RING, :], slots_d[j * P:(j + 1) * P, :]).then_inc(tokens_in[j % G_RING], 16)

            for k in range(STEP_RING):
                sp.wait_ge(rec_out[k], 16 * TOPK * len(range(k, B, STEP_RING)))
            for j in range(G_RING):
                load_tokens(j)
            spread_over = {k * 8 // 5: k for k in range(W_RING)}
            for j in range(NP - G_RING + 1):
                if j in spread_over:
                    k = spread_over[j]
                    sp.wait_ge(down_ok, j + 1)
                    load_weights(W_RING + k, k, w_next[k])
                if j + G_RING < NP:
                    sp.wait_ge(yg_ok, j + 1)
                    sp.wait_ge(y_ix_ok, j + 1)
                    load_tokens(j + G_RING)

            for k in range(Y_RING):
                sp.wait_ge(y_out[k], 16 * (NP // Y_RING))
            per = B // OUT_PARTS
            for c in range(OUT_PARTS):
                rows = y_d[c * per * L * TOPK:(c + 1) * per * L * TOPK, :].rearrange(
                    "(b l k) d -> l b (k d)", b=per, l=L)
                sp.dma_start(yk[:, c * per:(c + 1) * per, :], rows).then_inc(y_in[c], 16)
            for c in range(OUT_PARTS):
                if c in POOL_PARTS:
                    sp.wait_ge(pool_sum, POOL_PARTS.index(c) + 1)
                else:
                    sp.wait_ge(vector_sum, c + 1 - len([d for d in POOL_PARTS if d < c]))
                sp.dma_start(out[c * per:(c + 1) * per].rearrange("b l d -> l b d"),
                             x2[:, c * per:(c + 1) * per, :]).then_inc(out_sem, 16)
            sp.wait_ge(out_sem, OUT_PARTS * 16)

        @block.gpsimd
        def _(pool):
            pool.memset(ident[:, :], 0.0).then_inc(cleared, 1)
            pool.memset(neg_half[:, :], -0.5).then_inc(halves, 1)
            pool.wait_ge(cleared, 1)
            pool.affine_select(out=ident[:, :], in_=ident[:, :], compare_op=ALU.not_equal, fill=1.0,
                               base=0, pattern=[[-1, P]], channel_multiplier=1).then_inc(ident_ok, 1)
            pool.memset(ones[:, :], 1.0).then_inc(consts, 1)
            pool.wait_ge(halves, 1)
            pool.wait_ge(var_eps_ok, 1)
            pool.tensor_tensor(rstd[:, 0:HEAD], var_eps[:, 0:HEAD], neg_half[:, 0:HEAD], ALU.pow).then_inc(rstd_ok, 1)
            pool.wait_ge(wsim_in, 2 * 16)
            pool.wait_ge(consts, 1)
            pool.tensor_scalar(neg_w1[:, :], ones[:, :], wsim[:, 0:1], -1.0, ALU.mult, ALU.mult
                               ).then_inc(neg_w1_ok, 1)
            pool.tensor_scalar(neg_b[:, :], bsim[:, :], -1.0, None, ALU.mult).then_inc(neg_w1_ok, 1)
            pool.memset(earlier[:, :], 1.0).then_inc(consts, 1)
            pool.memset(ones_h[:, :], 1.0).then_inc(consts, 1)
            pool.memset(blank[:, :, :], 0.0).then_inc(blanked, 1)
            pool.iota(spare_i[:, :], pattern=[[P, NP]], base=SPARE, channel_multiplier=1).then_inc(blanked, 1)
            pool.wait_ge(blanked, 2)
            pool.tensor_copy(blank[:, :, D], spare_i[:, :]).then_inc(filled, 1)
            pool.wait_ge(var_eps_ok, 2)
            pool.tensor_tensor(rstd[:, HEAD:B], var_eps[:, HEAD:B], neg_half[:, HEAD:B], ALU.pow).then_inc(rstd_ok, 1)
            pool.memset(cx[:, :, :, D:D + 1], 1.0).then_inc(built, 1)
            pool.memset(seen[:, 0, :], 0.0).then_inc(consts, 1)
            pool.iota(trash_i[:, :], pattern=[[L, B * TOPK]], base=TRASH, channel_multiplier=1).then_inc(consts, 1)
            pool.iota(expert_i[:, :], pattern=[[1, E]], base=0, channel_multiplier=0).then_inc(consts, 1)
            pool.iota(y_no_i[:, :].rearrange("p (b k) -> p b k", k=TOPK), pattern=[[L * TOPK, B], [1, TOPK]],
                      base=0, channel_multiplier=TOPK).then_inc(consts, 1)
            pool.wait_ge(consts, 7)
            pool.memset(zeros[:, :], 0.0).then_inc(zeroed, 1)
            pool.affine_select(out=earlier[:, :], in_=earlier[:, :], compare_op=ALU.is_gt, fill=0.0,
                               base=0, pattern=[[1, L]], channel_multiplier=-1).then_inc(built, 1)
            pool.tensor_copy(trash_row[:, :], trash_i[:, :]).then_inc(built, 1)
            pool.tensor_copy(expert_no[:, :], expert_i[:, :]).then_inc(built, 1)
            pool.tensor_copy(y_no[:, :], y_no_i[:, :]).then_inc(built, 1)
            pool.wait_ge(const_in, 4 * 16)
            pool.wait_ge(x2_in, 16)
            pool.tensor_tensor(x2[:, :, :], x2[:, :, :],
                               bqv[:, :].unsqueeze(1).to_broadcast([L, B, D]), ALU.add).then_inc(x_bias, 1)
            pool.wait_ge(built, 5)

            def step(turn, r):
                s = STEP_RING * turn + r
                if there(s - 2):
                    pool.wait_ge(var_eps2_ok, s - 1)
                    pool.tensor_tensor(rstd2[:, :], var_eps2[:, :], neg_half[:, 0:1], ALU.pow).then_inc(rstd2_ok, 1)
                if there(s - 3):
                    b, k, next_k = s - 3, r % STEP_RING, (r + 1) % STEP_RING
                    pool.wait_ge(mask_ok, b + 1)
                    if past(s, 4):
                        pool.wait_ge(seen_ok, b)
                    pool.tensor_tensor(seen[:, next_k, :], seen[:, k, :], mask[:, :], ALU.add
                                       ).then_inc(seen_ok, 1)
                    if past(s, 6):
                        pool.wait_ge(rec_out[k], 16 * TOPK * (turn + (r - 3) // STEP_RING))
                    pool.tensor_copy(rows[:, k, :, D], y_no[:, bass.ds(TOPK * b, TOPK)]).then_inc(y_no_ok, 1)
                    pool.wait_ge(rows_init, 16 * ROW_FILLS)
                    pool.wait_ge(rows_ok, b + 1)
                    pool.wait_ge(y_no_ok, b + 1)
                    pool.wait_ge(slot_ok, b + 1)
                    pool.wait_ge(gate_ok, b + 1)
                    for c in range(TOPK):
                        pool.indirect_dma_start(
                            out=slots_d[:, :], out_offset=bass.IndirectOffsetOnAxis(ap=slot[:, k, c:c + 1], axis=0),
                            in_=rows[:, k, c, :], in_offset=None
                        ).then_inc(rec_out[k], 16)

            steps(pool, step)

            pool.wait_ge(y_init, 16 * Y_FILLS)

            def choose(j):
                if j >= 2:
                    pool.wait_ge(down_ok, j - 1)
                pool.tensor_copy(chooser[:, j % 2, :].rearrange("p (e s) -> p e s", e=2),
                                 ident[:, 2 * j:2 * j + 2].unsqueeze(2).to_broadcast([P, 2, CAP])
                                 ).then_inc(chooser_ok, 1)

            choose(0)
            for j in range(NP):
                if j + 1 < NP:
                    choose(j + 1)
                pool.wait_ge(tokens_in[j % G_RING], 16 * (j // G_RING + 1))
                pool.tensor_copy(y_ix[:, j:j + 1], xg[:, j % G_RING, D:D + 1]).then_inc(y_ix_ok, 1)
                pool.wait_ge(y_ix_ok, j + 1)
                pool.wait_ge(yg_ok, j + 1)
                pool.indirect_dma_start(
                    out=y_d[:, :], out_offset=bass.IndirectOffsetOnAxis(ap=y_ix[:, j:j + 1], axis=0),
                    in_=yg[:, j % Y_RING, :], in_offset=None).then_inc(y_out[j % Y_RING], 16)
            sum_parts(pool, POOL_PARTS, pool_part, pool_sum)

        @block.scalar
        def _(act):
            def step(turn, r):
                s = STEP_RING * turn + r
                if there(s - 1):
                    for g in range(GROUPS):
                        tiles = slice(g * PER * L, (g + 1) * PER * L)
                        act.wait_ge(shifted_ok[g], s)
                        if g == 0 and past(s, 2):
                            act.wait_ge(attn_ok, s - 1)
                        act.activation(probs[:, tiles], shifted[:, tiles], ACT.Exp).then_inc(probs_ok, 1)
                    act.wait_ge(neg_rmax_ok, s)
                    if past(s, 2):
                        act.wait_ge(hc_ok, s - 1)
                    act.activation(batt[:, :], neg_r[:, :], ACT.Exp, bias=neg_rmax[:, :], scale=-1.0,
                                   accum_out=batt_sum[:, :]).then_inc(batt_ok, 1)
                if past(s, 0) and there(s + 1):
                    if not past(s, 2):
                        act.wait_ge(lower_ok, s + 1)
                    act.wait_ge(enc_turned, s + 1)
                    norm_x(s + 1)
                if there(s - 2):
                    act.wait_ge(xln_turned, s - 1)
                    act.copy(xlnT[:, :], misc[:, 0:L]).then_inc(xlnT_ok, 1)
                if there(s - 1):
                    act.wait_ge(hc_ok, s)
                    if past(s, 2):
                        act.wait_ge(qv_ok, s - 1)
                    act.activation(enc_hc[:, :], encT[:, (r - 1) % STEP_RING, :], ACT.Copy, scale=hc_bar[:, :]
                                   ).then_inc(enc_hc_ok, 1)
                if there(s - 1):
                    act.wait_ge(inv_ok, s)
                    act.activation(hq[:, :], attn_bank[0:L, 0:D], ACT.Copy, scale=inv_sum[:, :]
                                   ).then_inc(hq_ok, 1)
                if there(s + 1):
                    act.wait_ge(ctx_turned[0], s + 2)
                    act.copy(cxT[:, 0:REM + 3 * P], turnA[:, 0:REM + 3 * P]).then_inc(cxT_ok[0], 1)
                    act.wait_ge(enc_turned, s + 2)
                    if past(s, 2):
                        act.wait_ge(qv_ok, s - 1)
                    act.copy(encT[:, (r + 1) % STEP_RING, :], misc[:, 0:L]).then_inc(encT_ok, 1)
                    act.activation(query[:, :], misc[:, 0:L], ACT.Identity, scale=wsim[:, 2:3], bias=wsim[:, 1:2]
                                   ).then_inc(query_ok, 1)
                if there(s - 1):
                    act.wait_ge(hq_turned, s)
                    act.copy(hqT[:, :], attn_bank[:, 0:L]).then_inc(hqT_ok, 1)
                if there(s):
                    act.wait_ge(spread, s + 1)
                    if past(s, 1):
                        act.wait_ge(neg_r_ok, s)
                    act.copy(shift[:, :], max_bank[:, 0:2 * L]).then_inc(shift_ok, 1)
                if there(s + 1):
                    act.wait_ge(ctx_turned[1], s + 2)
                    act.copy(cxT[:, REM + 3 * P:REM + 7 * P], turnB[:, :]).then_inc(cxT_ok[1], 1)
                    act.wait_ge(ctx_turned[2], s + 2)
                    act.copy(cxT[:, REM + 7 * P:S], turnA[:, :]).then_inc(cxT_ok[2], 1)
                if there(s - 2):
                    act.wait_ge(top_d_ok, s - 1)
                    if past(s, 3):
                        act.wait_ge(gate_ok, s - 2)
                    act.activation(gate_e[:, :], top_d[:, :], ACT.Exp, accum_out=gate_sum[:, :]
                                   ).then_inc(gate_e_ok, 1)
                    k = (r - 2) % STEP_RING
                    act.copy(rows[:, k, 1:TOPK, 0:D], rows[:, k, 0:1, 0:D].to_broadcast([L, TOPK - 1, D])
                             ).then_inc(rows_ok, 1)

            def norm_x(b):
                act.activation(enc[:, :], xs[:, bass.ds(b, 1), :].rearrange("p o d -> p (o d)"), ACT.Identity,
                               scale=rstd[:, bass.ds(b, 1)], bias=lower[:, bass.ds(b, 1)]).then_inc(enc_ok, 1)

            act.wait_ge(halves, 1)
            act.activation(table_junk[:, :], neg_half[:, 0:1], ACT.Exp).then_inc(table_there, 1)
            act.wait_ge(lower_ok, 1)
            norm_x(0)
            act.wait_ge(wsim_in, 2 * 16)
            steps(act, step)

            act.wait_ge(table_there, 1)
            act.activation(table_junk[:, :], neg_half[:, 0:1], ACT.Gelu).then_inc(table_there, 1)

            def ffn_step(turn, u):
                j = FFN_UNROLL * turn + u
                if there_pair(j + 2):
                    act.wait_ge(up_ok, j + 3)
                    if not isinstance(j, int) or j >= 0:
                        act.wait_ge(hidden_turned, j + 1)
                    act.copy(hidden[:, u % 2, :], up_bank[u % 2]).then_inc(up_kept, 1)
                if there_pair(j):
                    act.wait_ge(down_ok, j + 1)
                    if not isinstance(j, int) or j >= Y_RING:
                        act.wait_ge(y_out[u % Y_RING], 16 * (FFN_UNROLL // Y_RING * turn + u // Y_RING))
                    act.activation(yg[:, u % Y_RING, :], down_bank[u % 2][:, 0:D], ACT.Copy,
                                   scale=xg[:, u % G_RING, D + 1:W]).then_inc(yg_ok, 1)
                if there_pair(j + 2):
                    act.wait_ge(biased, j + 3)
                    act.activation(hiddenT[:, u % 2, :], hiddenT[:, u % 2, :], ACT.Gelu).then_inc(hidden_ok, 1)

            ffn_steps(act, ffn_step)

        @block.vector
        def _(dve):
            def lowered(batches):
                first, behind = batches[0], batches[-1] + 1
                dve.scalar_tensor_tensor(lower[:, first:behind], moments[:, first:behind, 0], -1.0,
                                         rstd[:, first:behind], ALU.mult, ALU.mult).then_inc(lower_ok, 1)

            dve.memset(b2_rows[E:P, :], 0.0).then_inc(b2_padded, 1)
            for batches, loaded in ((range(HEAD), x0_in), (range(HEAD, B), x_in)):
                first, behind = batches[0], batches[-1] + 1
                dve.wait_ge(loaded, 16)
                for b in batches:
                    dve.bn_stats(stats[:, b, :], xs[:, b, :]).then_inc(stats_ok, 1)
                for b in batches:
                    dve.wait_ge(stats_ok, b + 1)
                    dve.bn_aggr(moments[:, b, :], stats[:, b, :]).then_inc(moments_ok, 1)
                dve.wait_ge(moments_ok, behind)
                dve.tensor_scalar(var_eps[:, first:behind], moments[:, first:behind, 1], EPS, None, ALU.add
                                  ).then_inc(var_eps_ok, 1)
                if first == 0:
                    dve.wait_ge(rstd_ok, 1)
                    lowered(batches)
            dve.wait_ge(neg_w1_ok, 2)

            def step(turn, r):
                s = STEP_RING * turn + r
                routed, chosen = there(s - 2), there(s - 3)
                if routed:
                    if not past(s, 3):
                        dve.wait_ge(x_bias, 1)
                        dve.wait_ge(built, 5)
                    row = x2[:, bass.ds(s - 2, 1), :].rearrange("p o d -> p (o d)")
                    dve.wait_ge(qv_ok, s - 1)
                    dve.tensor_tensor(row, misc[0:L, 0:D], row, ALU.add).then_inc(x2_ok, 1)
                if chosen:
                    b = s - 3
                    dve.wait_ge(top_ix_ok, b + 1)
                    dve.tensor_copy(top_no[:, :], top_ix[:, 0:TOPK]).then_inc(top_no_ok, 1)
                if routed:
                    if in_loop(s):
                        dve.wait_ge(built, 5)
                    dve.wait_ge(x2_ok, s - 1)
                    dve.bn_stats(st2[:, :], row).then_inc(st2_ok, 1)
                if chosen:
                    dve.wait_ge(top_no_ok, b + 1)
                    dve.tensor_scalar(pick0[:, :], expert_no[:, :], top_no[:, 0:1], None, ALU.is_equal
                                      ).then_inc(pick0_ok, 1)
                if routed:
                    if in_loop(s):
                        dve.wait_ge(built, 5)
                    dve.wait_ge(st2_ok, s - 1)
                    dve.bn_aggr(mv2[:, :], st2[:, :]).then_inc(mv2_ok, 1)
                if chosen:
                    dve.wait_ge(pick0_ok, b + 1)
                    dve.scalar_tensor_tensor(pick01[:, :], expert_no[:, :], top_no[:, 1:2], pick0[:, :],
                                             ALU.is_equal, ALU.add).then_inc(pick01_ok, 1)
                if routed:
                    dve.wait_ge(mv2_ok, s - 1)
                    dve.tensor_scalar(var_eps2[:, :], mv2[:, 1:2], EPS, None, ALU.add).then_inc(var_eps2_ok, 1)
                if chosen:
                    dve.wait_ge(pick01_ok, b + 1)
                    if past(s, 4):
                        dve.wait_ge(seen_ok, b)
                    dve.scalar_tensor_tensor(mask[:, :], expert_no[:, :], top_no[:, 2:3], pick01[:, :],
                                             ALU.is_equal, ALU.add).then_inc(mask_ok, 1)
                    dve.wait_ge(gate_e_ok, b + 1)
                    dve.reciprocal(gate_inv[:, :], gate_sum[:, :]).then_inc(gate_inv_ok, 1)
                if there(s):
                    dve.wait_ge(sim_ok, s + 1)
                    if past(s, 1):
                        dve.wait_ge(max_turned, s)
                    dve.tensor_reduce(maxes[:, :],
                                      sim[:, :, 0:PER * L].rearrange("p g (t i) -> p i g t", t=PER),
                                      AX.XY, ALU.max).then_inc(maxes_ok, 1)
                if routed:
                    k = (r - 2) % STEP_RING
                    dve.wait_ge(rstd2_ok, s - 1)
                    if past(s, 5):
                        dve.wait_ge(rec_out[k], 16 * TOPK * (turn + (r - 2) // STEP_RING))
                    dve.tensor_scalar(rows[:, k, 0, 0:D], x2[:, bass.ds(s - 2, 1), :].rearrange("p o d -> p (o d)"),
                                      mv2[:, 0:1], rstd2[:, :], ALU.subtract, ALU.mult).then_inc(xln_ok, 1)
                if chosen:
                    dve.wait_ge(counted, b + 1)
                    for c in range(TOPK):
                        dve.scalar_tensor_tensor(pos_junk[:, c, :], expert_no[:, :], top_no[:, c:c + 1],
                                                 max_bank[0:L, 0:E], ALU.is_equal, ALU.mult,
                                                 accum_out=pos[:, c:c + 1]).then_inc(pos_ok, 1)
                if there(s - 1):
                    dve.wait_ge(batt_ok, s)
                    dve.tensor_tensor_reduce(hc_junk[:, :], batt[:, :], encT[:, (r - 1) % STEP_RING, :], 1.0, 0.0,
                                             ALU.mult, ALU.add, hc_raw[:, :]).then_inc(hc_raw_ok, 1)
                    dve.reciprocal(batt_inv[:, :], batt_sum[:, :]).then_inc(batt_inv_ok, 1)
                if chosen:
                    dve.wait_ge(pos_ok, TOPK * (b + 1))
                    dve.scalar_tensor_tensor(slot_b[:, :], top_no[:, :], float(CAP), pos[:, :],
                                             ALU.mult, ALU.add).then_inc(slot_b_ok, 1)
                    dve.scalar_tensor_tensor(over[:, :], pos[:, :], float(CAP),
                                             trash_row[:, bass.ds(TOPK * b, TOPK)],
                                             ALU.is_ge, ALU.mult).then_inc(over_ok, 1)
                if there(s - 1):
                    dve.wait_ge(hc_raw_ok, s)
                    dve.wait_ge(batt_inv_ok, s)
                    dve.tensor_tensor(hc_bar[:, :], hc_raw[:, :], batt_inv[:, :], ALU.mult).then_inc(hc_ok, 1)
                if chosen:
                    dve.wait_ge(gate_inv_ok, b + 1)
                    dve.tensor_scalar(rows[:, r % STEP_RING, :, D + 1], gate_e[:, :], gate_inv[:, :], None,
                                      ALU.mult).then_inc(gate_ok, 1)
                    dve.wait_ge(slot_b_ok, b + 1)
                    dve.wait_ge(over_ok, b + 1)
                    if past(s, 6):
                        dve.wait_ge(rec_out[r % STEP_RING], 16 * TOPK * (turn + (r - 3) // STEP_RING))
                    dve.tensor_tensor(slot[:, r % STEP_RING, :], slot_b[:, :], over[:, :], ALU.max
                                      ).then_inc(slot_ok, 1)
                if there(s - 1):
                    dve.wait_ge(attn_ok, s)
                    if past(s, 2):
                        dve.wait_ge(hq_ok, s - 1)
                    dve.reciprocal(inv_sum[:, :], attn_bank[0:L, D:D + 1]).then_inc(inv_ok, 1)
                if there(s):
                    dve.wait_ge(max_turned, s + 1)
                    dve.tensor_reduce(row_max[:, :], max_bank[0:L, 0:P], AX.X, ALU.max).then_inc(row_max_ok, 1)
                if routed:
                    dve.wait_ge(logits_raw, s - 1)
                    dve.tensor_tensor(logits[:, :], misc[0:L, 0:E], gateb[:, :], ALU.add).then_inc(logits_ok, 1)
                if there(s):
                    dve.wait_ge(row_max_ok, s + 1)
                    dve.tensor_scalar(neg_diag[:, :], ident[0:L, 0:L], row_max[:, :], -1.0, ALU.mult, ALU.mult
                                      ).then_inc(diag_ok, 1)
                if routed:
                    if in_loop(s):
                        dve.wait_ge(built, 5)
                    dve.wait_ge(logits_ok, s - 1)
                    dve.max(top[:, :], logits[:, :]).then_inc(top_ok, 1)
                    if in_loop(s):
                        dve.wait_ge(built, 5)
                    dve.wait_ge(top_ok, s - 1)
                    dve.max_index(top_ix[:, :], top[:, :], logits[:, :]).then_inc(top_ix_ok, 1)
                    if past(s, 3):
                        dve.wait_ge(gate_e_ok, s - 2)
                    dve.tensor_scalar(top_d[:, :], top[:, 0:TOPK], top[:, 0:1], None, ALU.subtract
                                      ).then_inc(top_d_ok, 1)
                if there(s - 1):
                    dve.wait_ge(hqT_ok, s)
                    dve.tensor_tensor(enc_hq[:, :], encT[:, (r - 1) % STEP_RING, :], hqT[:, :], ALU.mult
                                      ).then_inc(enc_hq_ok, 1)
                if there(s):
                    dve.wait_ge(shift_ok, s + 1)
                    if past(s, 1):
                        dve.wait_ge(probs_ok, GROUPS * s)
                    for g in range(GROUPS):
                        w = PER * L
                        dve.tensor_tensor(shifted[:, g * w:(g + 1) * w].rearrange("p (t i) -> p t i", t=PER),
                                          sim[:, g, 0:w].rearrange("p (t i) -> p t i", t=PER),
                                          shift[:, 0:L].unsqueeze(1).to_broadcast([P, PER, L]),
                                          ALU.add).then_inc(shifted_ok[g], 1)
                    if past(s, 1):
                        dve.wait_ge(batt_ok, s)
                    dve.scalar_tensor_tensor(neg_r[:, :], shift[:, 0:L], neg_b[:, :], shift[:, L:2 * L],
                                             ALU.add, ALU.add).then_inc(neg_r_ok, 1)
                if not past(s, 1) and s == 0:
                    dve.wait_ge(rstd_ok, 2)
                    lowered(range(HEAD, B))
                if there(s):
                    dve.wait_ge(neg_r_ok, s + 1)
                    dve.tensor_reduce(neg_rmax[:, :], neg_r[:, :], AX.X, ALU.min).then_inc(neg_rmax_ok, 1)

            steps(dve, step)

            dve.wait_ge(b_turned, 1)
            dve.tensor_copy(b1T[:, :].rearrange("p (j c e) -> p j c e", c=HC, e=2),
                            sim[:, 0, 0:HC * E].rearrange("p (c j e) -> p j c e", c=HC, e=2)).then_inc(b_kept, 1)
            def ffn_step(turn, u):
                j = FFN_UNROLL * turn + u
                if there_pair(j + 4):
                    k = u % 2
                    dve.wait_ge(xg_turned, j + 5)
                    if not isinstance(j, int) or j >= -2:
                        dve.wait_ge(up_ok, j + 3)
                    dve.tensor_copy(xgT[:, k, :], xg_bank[k][:, 0:P]).then_inc(xgT_ok, 1)
                if there_pair(j + 2):
                    dve.wait_ge(hidden_turned, j + 3)
                    if not isinstance(j, int) or j >= 0:
                        dve.wait_ge(down_ok, j + 1)
                    dve.tensor_tensor(hiddenT[:, u % 2, :].rearrange("p (g s) -> p g s", s=CAP),
                                      hT_bank[u % 2].rearrange("p (g s) -> p g s", s=CAP),
                                      b1T[:, bass.ds(2 * HC * (j + 2), 2 * HC)].unsqueeze(2)
                                      .to_broadcast([P, 2 * HC, CAP]), ALU.add).then_inc(biased, 1)

            ffn_steps(dve, ffn_step)

            sum_parts(dve, [c for c in range(OUT_PARTS) if c not in POOL_PARTS], vector_part, vector_sum)

        @block.tensor
        def _(pe):
            def turn_tiles(target, first, slots, k):
                for i in slots:
                    n = rows_of(i)
                    at = tile_cols(i).start - first
                    last = pe.transpose(target[:, at:at + n], cx[0:n, k, i, 0:D], ident[0:n, 0:n])
                return last

            def attend(slots, k, b):
                for i in slots:
                    if i % PER == 0:
                        pe.wait_ge(probs_ok, GROUPS * b + i // PER + 1)
                    n = rows_of(i)
                    last = pe.matmul(attn_bank[0:L, 0:D + 1], probs[0:n, i * L:(i + 1) * L],
                                     cx[0:n, k, i, :], start=(i == 0), stop=(i == TILES - 1))
                return last

            def step(turn, r):
                s = STEP_RING * turn + r
                old, now, new = (r - 1) % STEP_RING, r % STEP_RING, (r + 1) % STEP_RING
                if there(s):
                    pe.wait_ge(query_ok, s + 1)
                    for g in range(GROUPS):
                        pe.wait_ge(cxT_ok[g], s + 1)
                        if past(s, 1):
                            pe.wait_ge(shifted_ok[g], s)
                        for t in range(PER):
                            last = pe.matmul(sim[:, g, t * L:(t + 1) * L], cxT[:, tile_cols(g * PER + t)],
                                             query[:, :], start=True, stop=True)
                    last.then_inc(sim_ok, 1)
                if there(s - 1):
                    if past(s, 2):
                        pe.wait_ge(hqT_ok, s - 1)
                    else:
                        pe.wait_ge(built, 5)
                    attend(range(TILES // 2), old, s - 1)
                if there(s - 3):
                    b = s - 3
                    pe.wait_ge(mask_ok, b + 1)
                    if past(s, 4):
                        pe.wait_ge(seen_ok, b)
                    if there(s - 1):
                        pe.wait_ge(shift_ok, s)
                    else:
                        pe.wait_ge(pos_ok, TOPK * b)
                    pe.matmul(max_bank[0:L, 0:E], earlier[:, :], mask[:, :], start=True, stop=False)
                    pe.matmul(max_bank[0:L, 0:E], ones_h[:, :], seen[:, now, :],
                              start=False, stop=True).then_inc(counted, 1)
                if there(s - 1):
                    attend(range(TILES // 2, TILES), old, s - 1).then_inc(attn_ok, 1)
                if there(s - 2):
                    pe.wait_ge(xln_ok, s - 1)
                    pe.transpose(misc[:, 0:L], rows[:, (r - 2) % STEP_RING, 0, 0:D], ident[0:L, 0:L]
                                 ).then_inc(xln_turned, 1)
                if there(s):
                    pe.wait_ge(maxes_ok, s + 1)
                    if there(s - 3):
                        pe.wait_ge(pos_ok, TOPK * (s - 2))
                    elif past(s, 1):
                        pe.wait_ge(shift_ok, s)
                    pe.transpose(max_bank[0:L, 0:P], maxes[:, :], ident[:, :]).then_inc(max_turned, 1)
                if there(s + 1):
                    pe.wait_ge(ctx_in[new], 32 * (turn + (r + 1) // STEP_RING + 1))
                    if past(s, 0):
                        pe.wait_ge(cxT_ok[2], s + 1)
                    turn_tiles(turnA, 0, (1, 2, 3, 0), new).then_inc(ctx_turned[0], 1)
                if there(s - 2):
                    pe.wait_ge(xlnT_ok, s - 1)
                    if not past(s, 3):
                        pe.wait_ge(const_in, 4 * 16)
                    pe.matmul(misc[0:L, 0:E], xlnT[:, :], gatew[:, :], start=True, stop=True
                              ).then_inc(logits_raw, 1)
                if there(s + 1):
                    if past(s, 0):
                        pe.wait_ge(cxT_ok[1], s + 1)
                    turn_tiles(turnB, REM + 3 * P, range(PER, 2 * PER), new).then_inc(ctx_turned[1], 1)
                    pe.wait_ge(enc_ok, s + 2)
                    if there(s - 2):
                        pe.wait_ge(logits_ok, s - 1)
                    pe.transpose(misc[:, 0:L], enc[:, :], ident[0:L, 0:L]).then_inc(enc_turned, 1)
                if there(s - 1):
                    pe.wait_ge(hq_ok, s)
                    pe.transpose(attn_bank[:, 0:L], hq[:, :], ident[0:L, 0:L]).then_inc(hq_turned, 1)
                if there(s):
                    pe.wait_ge(diag_ok, s + 1)
                    pe.matmul(max_bank[:, 0:L], ones[0:L, :], neg_diag[:, :], start=True, stop=True)
                    pe.matmul(max_bank[:, L:2 * L], neg_w1[:, :], encT[:, now, :], start=True, stop=True
                              ).then_inc(spread, 1)
                if there(s + 1):
                    pe.wait_ge(cxT_ok[0], s + 2)
                    turn_tiles(turnA, REM + 7 * P, range(2 * PER, TILES), new).then_inc(ctx_turned[2], 1)
                if there(s - 1):
                    if there(s + 1):
                        pe.wait_ge(query_ok, s + 2)
                    else:
                        pe.wait_ge(logits_ok, s - 1)
                    if not past(s, 2):
                        pe.wait_ge(const_in, 4 * 16)
                    pe.matmul(misc[0:L, 0:D], encT[:, old, :], wqv[:, 0, :], start=True, stop=False)
                    pe.wait_ge(enc_hc_ok, s)
                    pe.matmul(misc[0:L, 0:D], enc_hc[:, :], wqv[:, 3, :], start=False, stop=False)
                    pe.wait_ge(hqT_ok, s)
                    pe.matmul(misc[0:L, 0:D], hqT[:, :], wqv[:, 1, :], start=False, stop=False)
                    pe.wait_ge(enc_hq_ok, s)
                    pe.matmul(misc[0:L, 0:D], enc_hq[:, :], wqv[:, 2, :], start=False, stop=True
                              ).then_inc(qv_ok, 1)

            pe.wait_ge(ident_ok, 1)
            pe.wait_ge(neg_w1_ok, 2)
            steps(pe, step)

            pe.wait_ge(bias_in, 32)
            pe.wait_ge(b2_padded, 1)
            for c in range(HC):
                last = pe.transpose(sim[:, 0, c * E:(c + 1) * E],
                                    b1_rows[:, :].rearrange("e (p c) -> e c p", c=HC)[:, c, :], ident[0:E, 0:E])
            last.then_inc(b_turned, 1)
            pe.wait_ge(b_kept, 1)

            def turn_tokens(j):
                pe.wait_ge(tokens_in[j % G_RING], 16 * (j // G_RING + 1))
                if j >= 2:
                    pe.wait_ge(xgT_ok, j - 1)
                pe.transpose(xg_bank[j % 2][:, 0:P], xg[:, j % G_RING, 0:D], ident[:, :]).then_inc(xg_turned, 1)

            def up(j):
                k = j % W_RING
                if j == 0:
                    pe.wait_ge(w_first, 32 * W_RING)
                if j >= W_RING:
                    pe.wait_ge(w_next[k], 32)
                pe.wait_ge(xgT_ok, j + 1)
                if j >= 2:
                    pe.wait_ge(up_kept, j - 1)
                for e in range(2):
                    own = slice(e * CAP, (e + 1) * CAP)
                    last = pe.matmul(up_bank[j % 2][own, :], xgT[:, j % 2, own], wring[:, k, 0, e],
                                     start=True, stop=True)
                last.then_inc(up_ok, 1)

            def turn_hidden(j):
                pe.wait_ge(up_kept, j + 1)
                if j >= 2:
                    pe.wait_ge(biased, j - 1)
                units = hidden[:, j % 2, :].rearrange("s (p c) -> s c p", c=HC)
                for c in range(HC):
                    last = pe.transpose(hT_bank[j % 2][:, c * P:(c + 1) * P], units[:, c, :], ident[:, :])
                last.then_inc(hidden_turned, 1)

            def down(j):
                pe.wait_ge(hidden_ok, j + 1)
                if j >= 2:
                    pe.wait_ge(yg_ok, j - 1)
                pe.wait_ge(chooser_ok, j + 1)
                pe.matmul(down_bank[j % 2][:, 0:D], chooser[:, j % 2, :], b2_rows[:, :], start=True, stop=False)
                for c in range(HC):
                    for e in range(2):
                        at = c * P + e * CAP
                        last = pe.matmul(down_bank[j % 2][e * CAP:(e + 1) * CAP, 0:D], hiddenT[:, j % 2, at:at + CAP],
                                         wring[:, j % W_RING, 1, e, c * D:(c + 1) * D],
                                         start=False, stop=(c == HC - 1))
                last.then_inc(down_ok, 1)

            for j in range(-5, NP):
                if j >= 0:
                    down(j)
                if 0 <= j + 2 < NP:
                    turn_hidden(j + 2)
                if 0 <= j + 3 < NP:
                    up(j + 3)
                if j + 5 < NP:
                    turn_tokens(j + 5)


_INS = ['x', 'ctx_1024', 'L0_xattn_w_sim', 'L0_xattn_b_sim', 'L0_xattn_W_qv', 'L0_xattn_b_qv', 'L0_ffn_gate_w',
        'L0_ffn_gate_b', 'L0_ffn_w1', 'L0_ffn_b1', 'L0_ffn_w2', 'L0_ffn_b2']


def kernel(**inputs):
    import numpy as np
    import concourse.bacc as bacc
    from concourse.bass_utils import run_bass_kernel_spmd

    nc = bacc.Bacc("TRN2", target_bir_lowering=False, num_devices=1)
    arrays, args = {}, []
    for name in _INS:
        a = np.ascontiguousarray(inputs[name])
        arrays[f"in_{name}"] = a
        args.append(nc.dram_tensor(f"in_{name}", a.shape, mybir.dt.from_np(a.dtype), kind="ExternalInput").ap())
    shape = inputs['x'].shape
    args.append(nc.dram_tensor("out_0", shape, F32, kind="ExternalOutput").ap())
    build_xattn_moe(nc, *args)
    result = run_bass_kernel_spmd(nc, [arrays], core_ids=[0])
    return result.results[0]["out_0"]
```
